# Optimizing a Trainium2 kernel written in Bass

```python
import numpy as np
import jax
import jax.numpy as jnp

def _softmax(x, axis=-1):
    return jax.nn.softmax(x, axis=axis)

def _gelu(x):
    return jax.nn.gelu(x, approximate=True)

def _silu(x):
    return jax.nn.silu(x)

def _sigmoid(x):
    return jax.nn.sigmoid(x)

def _layernorm(x, axis=-1, eps=1e-05):
    m = jnp.mean(x, axis=axis, keepdims=True)
    v = jnp.var(x, axis=axis, keepdims=True)
    return (x - m) / jnp.sqrt(v + eps)

def _scatter_add(tgt, idx, src, axis=0):
    return tgt.at[idx].add(src)

def _segment_sum(src, seg, n):
    return jax.ops.segment_sum(src, seg, n)
kernel_name = 'mk_xattn_ffn_d2_seqx_r4_0d88ba'

def setup_inputs(seed: int=0):
    np.random.seed(seed)
    _w = jnp.asarray

    def _rec_inputs():
        import jax
        import jax.numpy as jnp
        _rk = jax.random.key(seed)
        x = 6.313e-05 + 0.9998 * jax.random.normal(jax.random.fold_in(_rk, 1), (16, 256, 256), jnp.float32)
        _lenS = 256 - jax.random.randint(jax.random.fold_in(_rk, 7), (16,), 0, max(1, 256 // 4) + 1, jnp.int32)
        _lenS2 = 120 - jax.random.randint(jax.random.fold_in(_rk, 8), (16,), 0, max(1, 120 // 4) + 1, jnp.int32)
        _ctx_1024P = jax.random.normal(jax.random.fold_in(_rk, 11), (16, 16, 256), jnp.float32)
        _ctx_1024c = jax.random.dirichlet(jax.random.fold_in(_rk, 511), 0.3 * jnp.ones((16,), jnp.float32), (16, 120))
        _ctx_1024t = jnp.einsum('bsk,bkd->bsd', _ctx_1024c, _ctx_1024P)
        _ctx_1024t = _ctx_1024t * jax.lax.rsqrt(jnp.mean(jnp.square(_ctx_1024t)) + 1e-12) * 0.953939
        ctx_1024 = -0.000214406 + 1.00034 * (_ctx_1024t + 0.3 * jax.random.normal(jax.random.fold_in(_rk, 611), (16, 120, 256), jnp.float32))
        return (x, ctx_1024)
    x, ctx_1024 = _rec_inputs()

    def _L0_xattn_setup():
        import jax, jax.numpy as jnp
        import numpy as np
        from jax import lax
        BIG = jnp.float32(1e+30)

        def _pairwise_euclidean(a, b):
            aa = jnp.sum(a * a, axis=-1)[:, None]
            bb = jnp.sum(b * b, axis=-1)[None, :]
            ab = a @ b.T
            return jnp.sqrt(jnp.maximum(aa + bb - 2.0 * ab, 0.0))

        def _dtw_cost(D):
            row0 = jnp.cumsum(D[0])

            def row_step(prev_row, d_row):
                first = d_row[0] + prev_row[0]

                def col_step(left, inp):
                    d_ij, up, diag = inp
                    r = d_ij + jnp.minimum(jnp.minimum(up, left), diag)
                    return (r, r)
                _, rest = lax.scan(col_step, first, (d_row[1:], prev_row[1:], prev_row[:-1]))
                row = jnp.concatenate([first[None], rest])
                return (row, row)
            _, rows = lax.scan(row_step, row0, D[1:])
            return jnp.concatenate([row0[None], rows], axis=0)

        def _backtrack(R, T1, T2):
            L = T1 + T2 - 1

            def step(carry, _):
                i, j, done = carry
                valid = jnp.logical_not(done)
                cd = jnp.where((i > 0) & (j > 0), R[jnp.maximum(i - 1, 0), jnp.maximum(j - 1, 0)], BIG)
                cu = jnp.where(i > 0, R[jnp.maximum(i - 1, 0), j], BIG)
                cl = jnp.where(j > 0, R[i, jnp.maximum(j - 1, 0)], BIG)
                choice = jnp.argmin(jnp.stack([cd, cu, cl]))
                ni = jnp.where(choice <= 1, i - 1, i)
                nj = jnp.where((choice == 0) | (choice == 2), j - 1, j)
                at_origin = (i == 0) & (j == 0)
                ni = jnp.where(at_origin, 0, ni)
                nj = jnp.where(at_origin, 0, nj)
                return ((ni, nj, done | at_origin), (i, j, valid))
            init = (jnp.int32(T1 - 1), jnp.int32(T2 - 1), jnp.bool_(False))
            _, (i_idx, j_idx, valid) = lax.scan(step, init, None, length=L)
            return (i_idx, j_idx, valid)

        def _align_one(small, large):
            T_small, d = small.shape
            T_large = large.shape[0]
            D = _pairwise_euclidean(small, large)
            R = _dtw_cost(D)
            i_idx, j_idx, valid = _backtrack(R, T_small, T_large)
            contrib = small[i_idx] * valid[:, None].astype(small.dtype)
            expanded = jnp.zeros((T_large, d), dtype=small.dtype).at[j_idx].add(contrib)
            return expanded
        key = jax.random.key(seed)
        k1, k2 = jax.random.split(key)
        teacher = jax.random.normal(k1, (16, 100, 256), dtype=jnp.float32)
        student = jax.random.normal(k2, (16, 150, 256), dtype=jnp.float32)
        return {'teacher_features': teacher, 'student_features': student}
    _L0_xattn_all = _L0_xattn_setup()
    _L0_xattn_in = {k: v for k, v in _L0_xattn_all.items() if k in ()}
    del _L0_xattn_all

    def _L0_ffn_setup():
        import jax, jax.numpy as jnp
        import numpy as np
        HIDDEN = 256
        INNER = 1024

        def _weight_quant(w):
            scale = 1.0 / jnp.clip(jnp.mean(jnp.abs(w)), 1e-05)
            wq = jnp.clip(jnp.round(w * scale), -1.0, 1.0) / scale
            return w + jax.lax.stop_gradient(wq - w)

        def _act_quant(x):
            scale = 127.0 / jnp.clip(jnp.max(jnp.abs(x), axis=-1, keepdims=True), 1e-05)
            xq = jnp.clip(jnp.round(x * scale), -128.0, 127.0) / scale
            return x + jax.lax.stop_gradient(xq - x)

        def _bitlinear(x, w):
            return jnp.einsum('bsi,oi->bso', _act_quant(x), _weight_quant(w))
        key = jax.random.key(seed)
        k0, k1, k2, k3 = jax.random.split(key, 4)
        x = jax.random.normal(k0, (4, 512, HIDDEN), dtype=jnp.float32)
        w_gate = jax.random.normal(k1, (INNER, HIDDEN), dtype=jnp.float32) / np.sqrt(HIDDEN)
        w_up = jax.random.normal(k2, (INNER, HIDDEN), dtype=jnp.float32) / np.sqrt(HIDDEN)
        w_down = jax.random.normal(k3, (HIDDEN, INNER), dtype=jnp.float32) / np.sqrt(INNER)
        return {'x': x, 'w_gate': w_gate, 'w_up': w_up, 'w_down': w_down}
    _L0_ffn_all = _L0_ffn_setup()
    _L0_ffn_in = {k: v for k, v in _L0_ffn_all.items() if k in ('w_gate', 'w_up', 'w_down')}
    del _L0_ffn_all

    def _L1_xattn_setup():
        import jax, jax.numpy as jnp
        import numpy as np
        HEADS = 8
        DIM_HEAD = 64
        key = jax.random.key(seed)
        ks = jax.random.split(key, 9)
        B, N1, N2, D = (4, 512, 512, 256)
        inner = HEADS * DIM_HEAD
        s_in = 1.0 / np.sqrt(D)
        s_inner = 1.0 / np.sqrt(inner)
        return {'x1': jax.random.normal(ks[0], (B, N1, D), jnp.float32), 'x2': jax.random.normal(ks[1], (B, N2, D), jnp.float32), 'Wq1': jax.random.normal(ks[2], (D, inner), jnp.float32) * s_in, 'Wk1': jax.random.normal(ks[3], (D, inner), jnp.float32) * s_in, 'Wv1': jax.random.normal(ks[4], (D, inner), jnp.float32) * s_in, 'Wk2': jax.random.normal(ks[5], (D, inner), jnp.float32) * s_in, 'Wv2': jax.random.normal(ks[6], (D, inner), jnp.float32) * s_in, 'Wo': jax.random.normal(ks[7], (inner, D), jnp.float32) * s_inner, 'bo': jnp.zeros((D,), jnp.float32)}
    _L1_xattn_all = _L1_xattn_setup()
    _L1_xattn_in = {k: v for k, v in _L1_xattn_all.items() if k in ('Wq1', 'Wk1', 'Wv1', 'Wk2', 'Wv2', 'Wo', 'bo')}
    del _L1_xattn_all

    def _L1_ffn_setup():
        import jax, jax.numpy as jnp
        import numpy as np
        T, Z, D_DIM = (8, 512, 256)
        N_EXP, P_SLOT, H = (64, 32, 256)
        LN_EPS = 1e-05
        key = jax.random.key(seed)
        k = jax.random.split(key, 5)
        s = 0.02
        return {'x': jax.random.normal(k[0], (T, Z, D_DIM), dtype=jnp.float32), 'phi_w': jax.random.normal(k[1], (N_EXP * P_SLOT, D_DIM), dtype=jnp.float32) * s, 'phi_b': jax.random.normal(k[2], (N_EXP * P_SLOT,), dtype=jnp.float32) * s, 'expert_w': jax.random.normal(k[3], (N_EXP, D_DIM, H), dtype=jnp.float32) * s, 'expert_b': jax.random.normal(k[4], (N_EXP, H), dtype=jnp.float32) * s}
    _L1_ffn_all = _L1_ffn_setup()
    _L1_ffn_in = {k: v for k, v in _L1_ffn_all.items() if k in ('phi_w', 'phi_b', 'expert_w', 'expert_b')}
    del _L1_ffn_all
    return {'x': x, 'ctx_1024': ctx_1024, 'L0_ffn_w_gate': _L0_ffn_in['w_gate'], 'L0_ffn_w_up': _L0_ffn_in['w_up'], 'L0_ffn_w_down': _L0_ffn_in['w_down'], 'L1_xattn_Wq1': _L1_xattn_in['Wq1'], 'L1_xattn_Wk1': _L1_xattn_in['Wk1'], 'L1_xattn_Wv1': _L1_xattn_in['Wv1'], 'L1_xattn_Wk2': _L1_xattn_in['Wk2'], 'L1_xattn_Wv2': _L1_xattn_in['Wv2'], 'L1_xattn_Wo': _L1_xattn_in['Wo'], 'L1_xattn_bo': _L1_xattn_in['bo'], 'L1_ffn_phi_w': _L1_ffn_in['phi_w'], 'L1_ffn_phi_b': _L1_ffn_in['phi_b'], 'L1_ffn_expert_w': _L1_ffn_in['expert_w'], 'L1_ffn_expert_b': _L1_ffn_in['expert_b']}

def reference(x, ctx_1024, L0_ffn_w_gate, L0_ffn_w_up, L0_ffn_w_down, L1_xattn_Wq1, L1_xattn_Wk1, L1_xattn_Wv1, L1_xattn_Wk2, L1_xattn_Wv2, L1_xattn_Wo, L1_xattn_bo, L1_ffn_phi_w, L1_ffn_phi_b, L1_ffn_expert_w, L1_ffn_expert_b):
    import jax
    import jax.numpy as jnp

    def _L0_xattn_ref(teacher_features, student_features):
        import jax, jax.numpy as jnp
        import numpy as np
        from jax import lax
        BIG = jnp.float32(1e+30)

        def _pairwise_euclidean(a, b):
            aa = jnp.sum(a * a, axis=-1)[:, None]
            bb = jnp.sum(b * b, axis=-1)[None, :]
            ab = a @ b.T
            return jnp.sqrt(jnp.maximum(aa + bb - 2.0 * ab, 0.0))

        def _dtw_cost(D):
            row0 = jnp.cumsum(D[0])

            def row_step(prev_row, d_row):
                first = d_row[0] + prev_row[0]

                def col_step(left, inp):
                    d_ij, up, diag = inp
                    r = d_ij + jnp.minimum(jnp.minimum(up, left), diag)
                    return (r, r)
                _, rest = lax.scan(col_step, first, (d_row[1:], prev_row[1:], prev_row[:-1]))
                row = jnp.concatenate([first[None], rest])
                return (row, row)
            _, rows = lax.scan(row_step, row0, D[1:])
            return jnp.concatenate([row0[None], rows], axis=0)

        def _backtrack(R, T1, T2):
            L = T1 + T2 - 1

            def step(carry, _):
                i, j, done = carry
                valid = jnp.logical_not(done)
                cd = jnp.where((i > 0) & (j > 0), R[jnp.maximum(i - 1, 0), jnp.maximum(j - 1, 0)], BIG)
                cu = jnp.where(i > 0, R[jnp.maximum(i - 1, 0), j], BIG)
                cl = jnp.where(j > 0, R[i, jnp.maximum(j - 1, 0)], BIG)
                choice = jnp.argmin(jnp.stack([cd, cu, cl]))
                ni = jnp.where(choice <= 1, i - 1, i)
                nj = jnp.where((choice == 0) | (choice == 2), j - 1, j)
                at_origin = (i == 0) & (j == 0)
                ni = jnp.where(at_origin, 0, ni)
                nj = jnp.where(at_origin, 0, nj)
                return ((ni, nj, done | at_origin), (i, j, valid))
            init = (jnp.int32(T1 - 1), jnp.int32(T2 - 1), jnp.bool_(False))
            _, (i_idx, j_idx, valid) = lax.scan(step, init, None, length=L)
            return (i_idx, j_idx, valid)

        def _align_one(small, large):
            T_small, d = small.shape
            T_large = large.shape[0]
            D = _pairwise_euclidean(small, large)
            R = _dtw_cost(D)
            i_idx, j_idx, valid = _backtrack(R, T_small, T_large)
            contrib = small[i_idx] * valid[:, None].astype(small.dtype)
            expanded = jnp.zeros((T_large, d), dtype=small.dtype).at[j_idx].add(contrib)
            return expanded
        return jax.vmap(_align_one)(teacher_features, student_features)

    def _L0_ffn_ref(x, w_gate, w_up, w_down):
        import jax, jax.numpy as jnp
        import numpy as np
        HIDDEN = 256
        INNER = 1024

        def _weight_quant(w):
            scale = 1.0 / jnp.clip(jnp.mean(jnp.abs(w)), 1e-05)
            wq = jnp.clip(jnp.round(w * scale), -1.0, 1.0) / scale
            return w + jax.lax.stop_gradient(wq - w)

        def _act_quant(x):
            scale = 127.0 / jnp.clip(jnp.max(jnp.abs(x), axis=-1, keepdims=True), 1e-05)
            xq = jnp.clip(jnp.round(x * scale), -128.0, 127.0) / scale
            return x + jax.lax.stop_gradient(xq - x)

        def _bitlinear(x, w):
            return jnp.einsum('bsi,oi->bso', _act_quant(x), _weight_quant(w))
        gate = jax.nn.silu(_bitlinear(x, w_gate))
        up = _bitlinear(x, w_up)
        return _bitlinear(gate * up, w_down)

    def _L1_xattn_ref(x1, x2, Wq1, Wk1, Wv1, Wk2, Wv2, Wo, bo):
        import jax, jax.numpy as jnp
        import numpy as np
        HEADS = 8
        DIM_HEAD = 64
        h, d = (HEADS, DIM_HEAD)
        scale = d ** (-0.5)
        B, N1, _ = x1.shape
        N2 = x2.shape[1]

        def split_heads(t, n):
            return t.reshape(B, n, h, d)
        q1 = split_heads(x1 @ Wq1, N1)
        k1 = split_heads(x1 @ Wk1, N1)
        v1 = split_heads(x1 @ Wv1, N1)
        k2 = split_heads(x2 @ Wk2, N2)
        v2 = split_heads(x2 @ Wv2, N2)
        k = jnp.concatenate([k1, k2], axis=1)
        v = jnp.concatenate([v1, v2], axis=1)
        sim = jnp.einsum('bihd,bjhd->bhij', q1.astype(jnp.float32), k.astype(jnp.float32)) * scale
        attn = jax.nn.softmax(sim, axis=-1)
        out = jnp.einsum('bhij,bjhd->bihd', attn, v)
        out = out.reshape(B, N1, h * d)
        return out @ Wo + bo

    def _L1_ffn_ref(x, phi_w, phi_b, expert_w, expert_b):
        import jax, jax.numpy as jnp
        import numpy as np
        T, Z, D_DIM = (8, 512, 256)
        N_EXP, P_SLOT, H = (64, 32, 256)
        LN_EPS = 1e-05
        t, z, d = x.shape
        n = expert_w.shape[0]
        p = phi_w.shape[0] // n
        logits = (jnp.einsum('tzd,ed->tze', x, phi_w) + phi_b).reshape(t, z, n, p)
        D = jax.nn.softmax(logits, axis=3)
        C = jax.nn.softmax(logits, axis=2)
        X_tilde = jnp.einsum('tznp,tzd->npd', D, x)
        X_tilde = jnp.clip(X_tilde, -33000.0, 65000.0)
        mu = jnp.mean(X_tilde, axis=-1, keepdims=True)
        var = jnp.mean(jnp.square(X_tilde - mu), axis=-1, keepdims=True)
        X_tilde = (X_tilde - mu) * jax.lax.rsqrt(var + LN_EPS)
        X_tilde = jnp.tanh(X_tilde)
        Y_tilde = jnp.einsum('npd,ndH->npH', X_tilde, expert_w) + expert_b[:, None, :]
        Y = jnp.einsum('tznp,npH->tzH', C, Y_tilde)
        return Y
    x = x + _L0_xattn_ref(ctx_1024, _layernorm(x, axis=-1))
    x = x + _L0_ffn_ref(_layernorm(x, axis=-1), L0_ffn_w_gate, L0_ffn_w_up, L0_ffn_w_down)
    x = x + _L1_xattn_ref(_layernorm(x, axis=-1), ctx_1024, L1_xattn_Wq1, L1_xattn_Wk1, L1_xattn_Wv1, L1_xattn_Wk2, L1_xattn_Wv2, L1_xattn_Wo, L1_xattn_bo)
    x = x + _L1_ffn_ref(_layernorm(x, axis=-1), L1_ffn_phi_w, L1_ffn_phi_b, L1_ffn_expert_w, L1_ffn_expert_b)
    return x

_drawn_inputs = setup_inputs


def setup_inputs(seed=0):
    import zlib

    import numpy as np

    out = dict(_drawn_inputs(seed))
    spreads = {'L1_xattn_bo': (0.0, 0.1)}
    factors = {'L1_ffn_phi_b': 35.646}
    for name, (base, spread) in spreads.items():
        noise = np.random.default_rng([zlib.crc32(name.encode()), seed]).standard_normal(out[name].shape)
        drawn = base * np.exp(spread * noise) if base else spread * noise
        out[name] = jnp.asarray(drawn.astype(out[name].dtype))
    for name, factor in factors.items():
        out[name] = (out[name] * factor).astype(out[name].dtype)
    return out
```

```python
from contextlib import ExitStack

import concourse.bass as bass
from concourse import mybir

ALU = mybir.AluOpType
ACT = mybir.ActivationFunctionType
F32 = mybir.dt.float32
F16 = mybir.dt.float16
BF16 = mybir.dt.bfloat16
AX = mybir.AxisListType

P = 128
B, S, D = 16, 256, 256
T = B * S // P
DC = D // P
I = 120
INNER = 1024
HEADS, DH = 8, 64
HD = HEADS * DH
KEYS = S + I
NE, PS = 64, 32
SLOTS = NE * PS
LN_EPS = 1e-5
BIG = 1e30
ROUND = 12582912.0

BLK = 7
BW = 37
LANES = 8
STEPS = I + BLK - 1


class Steps:

    def __init__(self, eng, sem):
        self.eng, self.sem, self.n = eng, sem, 0

    def did(self, ins):
        ins.then_inc(self.sem, 1)
        self.n = self.n + 1

    def seen(self):
        self.eng.wait_ge(self.sem, self.n)

    def then(self, ins):
        self.did(ins)
        self.seen()

    def rounds(self, start, i, each):
        self.n = start + i * each


def hold(eng, sem, value):
    eng.wait_ge(sem, value)
    eng.wait_ge(sem, 1)


def moments(own, dve, stats, mv, tmp):
    even, odd, mean, var = stats[:, :, 1], stats[:, :, 4], mv[:, :, 0], mv[:, :, 1]
    own.did(dve.tensor_tensor(mean, even, odd, ALU.add))
    own.did(dve.tensor_tensor(tmp, even, odd, ALU.subtract))
    own.then(dve.tensor_tensor(var, stats[:, :, 2], stats[:, :, 5], ALU.add))
    own.did(dve.tensor_scalar(mean, mean, 0.5, None, ALU.mult))
    own.then(dve.tensor_tensor(tmp, tmp, tmp, ALU.mult))
    own.then(dve.tensor_scalar(tmp, tmp, 0.25, None, ALU.mult))
    own.then(dve.scalar_tensor_tensor(out=var, in0=var, scalar=1.0 / D, in1=tmp, op0=ALU.mult, op1=ALU.add))


def pairs(eng, n, body):
    body(0, 0, 0, False)
    body(1, 1, 0, False)
    with eng.Fori(1, n // 2) as i:
        body(2 * i, 0, i, True)
        body(2 * i + 1, 1, i, True)


def staged(eng, n, *stages, unroll=2):
    deepest = max(lag for lag, _ in stages)
    head = -(-(deepest + unroll) // unroll) * unroll

    def static(j):
        for lag, body in stages:
            b = j - lag
            if 0 <= b < n:
                body(b, b % unroll, b // unroll, b >= unroll)
    for j in range(head):
        static(j)
    with eng.Fori(head // unroll, n // unroll) as i:
        for at in range(unroll):
            for lag, body in stages:
                body(unroll * i + (at - lag), (at - lag) % unroll, i + (at - lag) // unroll, True)
    for j in range(n, n + deepest):
        static(j)


def late(b, least):
    return not isinstance(b, int) or b >= least


def block_width(k):
    return min(BW, S - k * BW)


def program(nc, x, ctx, ctxT, w_gateT, w_upT, w_downT, wq1, wk1, wv1, wk2, wv2, wo, bo, phiT, phi_b,
            expert_w, expert_b, ident_c, lane_start_c, path_end_c, head_sel_c, consts, out, stop):
    cost_d = nc.dram_tensor("cost_d", [B, I, S], F32, kind="Internal").ap()
    path_d = nc.dram_tensor("path_d", [B, I, S], F32, kind="Internal").ap()
    with ExitStack() as top:
        resid = top.enter_context(nc.sbuf_tensor("resid", [P, T, D], F32))
        ident = top.enter_context(nc.sbuf_tensor("ident", [P, P], F32))
        psum = top.enter_context(nc.psum_tensor("psum", [P, 8, 512], F32))
        ps = [psum[:, i, :] for i in range(8)]
        mv = top.enter_context(nc.sbuf_tensor("mv", [P, T, 2], F32))
        stats = top.enter_context(nc.sbuf_tensor("stats", [P, T, 6], F32))
        x_in = top.enter_context(nc.semaphore("x_in"))
        roots = [top.enter_context(nc.semaphore(name)) for name in ("var_ready", "std_ready")]
        align(nc, ps, resid, mv, stats, ident, roots, x_in, x, ctx, ctxT, ident_c, lane_start_c, path_end_c, cost_d, path_d)
        if stop != 1:
            ffn(nc, psum, resid, mv, stats, ident, roots, w_gateT, w_upT, w_downT)
        if stop not in (1, 2):
            attention(nc, psum, resid, mv, stats, ident, roots, ctxT, wq1, wk1, wv1, wk2, wv2, wo, bo, head_sel_c)
        if stop == 0:
            moe(nc, psum, resid, mv, stats, ident, roots, phiT, phi_b, expert_w, expert_b, consts, out)
            return
        done = top.enter_context(nc.semaphore("out_written"))
        with nc.Block() as block:
            @block.sync
            def _(sp):
                sp.dma_start(out.rearrange("b (h p) d -> p (b h) d", p=P), resid[:]).then_inc(done, 16)
                sp.wait_ge(done, 16)


def shift_lanes(dve, out, src, by):
    inside = [LANES - 1 if n == LANES - 1 else (n + by) % LANES for n in range(LANES)]
    return dve.stream_shuffle(out, src, [base + n for base in range(0, 32, LANES) for n in inside])


def rstd_root(act, roots, nth, var, root):
    var_ready, root_ready = roots
    act.wait_ge(var_ready, nth)
    act.activation(root, var, ACT.Sqrt).then_inc(root_ready, 1)


def rstd_of(own, dve, roots, nth, var, root, rstd, tmp):
    var_ready, root_ready = roots
    dve.tensor_scalar(var, var, LN_EPS, None, ALU.add).then_inc(var_ready, 1)
    dve.wait_ge(var_ready, nth)
    dve.wait_ge(root_ready, nth)
    own.then(dve.reciprocal(rstd, root))
    own.then(dve.tensor_tensor(tmp, rstd, rstd, ALU.mult))
    own.then(dve.tensor_tensor(tmp, tmp, var, ALU.mult))
    own.then(dve.tensor_scalar(tmp, tmp, -0.5, 1.5, ALU.mult, ALU.add))
    own.then(dve.tensor_tensor(rstd, rstd, tmp, ALU.mult))


def align(nc, ps, resid, mv, stats, ident, roots, x_in, x, ctx, ctxT, ident_c, lane_start_c, path_end_c, cost_d, path_d):
    with ExitStack() as c:
        def sb(name, shape, dt=F32):
            return c.enter_context(nc.sbuf_tensor(name, shape, dt))

        def sem(name):
            return c.enter_context(nc.semaphore(name))

        ones = sb("ones", [P, I])
        rstd = sb("rstd", [P, T])
        rtmp = sb("rtmp", [P, T])
        rroot = sb("rroot", [P, T])
        xn = sb("xn", [P, 2, 2, D])
        xnT = sb("xnT", [P, 2, DC, S])
        xsq = sb("xsq", [P, 2, DC, S])
        ctxb = sb("ctxb", [P, 2, D])
        ctxTb = sb("ctxTb", [P, 2, DC, I])
        csq = sb("csq", [P, D])
        scr = sb("scr", [P, 2, S])
        aa = sb("aa", [P, 2])
        d2 = sb("d2", [P, 2, S])
        root = sb("root", [P, 2, S])
        dist = sb("dist", [P, 2, S])
        cost = sb("cost", [P, STEPS, BW])
        acc = sb("acc", [P, STEPS + 1, BW + 1])
        row = sb("row", [P, 2, BW + 1])
        least = sb("least", [P, BW])
        pick = sb("pick", [P, STEPS, 2, BW], BF16)
        left = sb("left", [P, STEPS, BW + 1], BF16)
        tie = sb("tie", [P, STEPS, BW], BF16)
        marks = sb("marks", [P, 2, BW + 1])
        flow = sb("flow", [P, 2, BW + 2])
        inflow = sb("inflow", [P, BW + 1])
        edge = sb("edge", [P, 1])
        path = sb("path", [P, STEPS, BW])
        maskb = sb("maskb", [P, 2, S])

        consts_in, ctx_in, start_in = sem("consts_in"), [sem(f"ctx_in{n}") for n in range(2)], sem("start_in")
        ones_set, cost_set = sem("ones_set"), sem("cost_set")
        xn_ready, xnT_psum, xnT_ready = sem("xn_ready"), sem("xnT_psum"), sem("xnT_ready")
        dots_psum, aa_ready, d2_ready, root_ready, dist_ready = (
            sem("dots_psum"), sem("aa_ready"), sem("d2_ready"), sem("root_ready"), sem("dist_ready"))
        cost_out, cost_in = [sem(f"cost_out{n}") for n in range(2)], sem("cost_in")
        row_ready, row_saved, mark_ready, mark_saved = (
            sem("row_ready"), sem("row_saved"), sem("mark_ready"), sem("mark_saved"))
        path_out, mask_in, gathered, resid_ready = (
            sem("path_out"), [sem(f"mask_in{n}") for n in range(2)], sem("gathered"), sem("resid_ready"))
        dve_steps = sem("dve_steps")

        xt_ps = [ps[0], ps[1]]
        dot_ps = [ps[2], ps[3]]

        with nc.Block() as block:
            @block.sync
            def _(sp):
                for q in range(4):
                    sp.dma_start(resid[:, 8 * q:8 * q + 8, :],
                                 x.rearrange("b (h p) d -> p (b h) d", p=P)[:, 8 * q:8 * q + 8, :]).then_inc(x_in, 16)
                sp.dma_start(ident[:], ident_c).then_inc(consts_in, 16)
                sp.dma_start(row[:, 0, 0:1], lane_start_c).then_inc(start_in, 16)
                sp.dma_start(inflow[:], path_end_c).then_inc(start_in, 16)

                def load(b, par, r, again):
                    if again:
                        sp.wait_ge(dots_psum, b - 1)
                        sp.wait_ge(aa_ready, b - 1)
                    sp.dma_start(ctxb[0:I, par, :], ctx[b]).then_inc(ctx_in[par], 16)
                    sp.dma_start(ctxTb[:, par], ctxT[b].rearrange("(c p) i -> p c i", p=P)).then_inc(ctx_in[par], 16)
                pairs(sp, B, load)

            @block.gpsimd
            def _(pool):
                pool.memset(cost[:], BIG).then_inc(cost_set, 1)

                def store(b, par, r, again):
                    pool.wait_ge(dist_ready, b + 1)
                    pool.dma_start(cost_d[b], dist[0:I, par, :]).then_inc(cost_out[par], 16)
                pairs(pool, B, store)
                pool.wait_ge(cost_set, 1)
                for par in range(2):
                    pool.wait_ge(cost_out[par], 16 * B // 2)
                for k in range(BLK):
                    w = block_width(k)
                    pool.dma_start(cost[BLK - 1 - k:P:LANES, k:k + I, 0:w],
                                   cost_d[:, :, k * BW:k * BW + w]).then_inc(cost_in, 16)
                pool.wait_ge(mark_saved, STEPS)
                for k in range(BLK):
                    w = block_width(k)
                    pool.dma_start(path_d[:, :, k * BW:k * BW + w],
                                   path[BLK - 1 - k:P:LANES, k:k + I, 0:w]).then_inc(path_out, 16)
                pool.wait_ge(path_out, 16 * BLK)

                def masks(b, par, r, again):
                    if again:
                        pool.wait_ge(gathered, b - 1)
                    pool.dma_start(maskb[0:I, par, :], path_d[b]).then_inc(mask_in[par], 16)
                    pool.dma_start(ctxb[0:I, par, :], ctx[b]).then_inc(mask_in[par], 16)
                pairs(pool, B, masks)

            @block.tensor
            def _(pe):
                pe.wait_ge(consts_in, 16)
                pe.wait_ge(ones_set, 1)

                def products(b, par, r, again):
                    pe.wait_ge(xn_ready, 2 * b + 2)
                    for h in range(2):
                        for k in range(DC):
                            ins = pe.transpose(xt_ps[par][:, k * S + h * P:k * S + (h + 1) * P],
                                               xn[:, par, h, k * P:(k + 1) * P], ident[:])
                    ins.then_inc(xnT_psum, 1)
                    pe.wait_ge(ctx_in[par], (r + 1) * 32)
                    pe.wait_ge(xnT_ready, (b + 1) * 2)
                    if again:
                        pe.wait_ge(d2_ready, b - 1)
                    for k in range(DC):
                        pe.matmul(dot_ps[par][0:I, 0:S], ctxTb[:, par, k, :], xnT[:, par, k, :],
                                  start=(k == 0), stop=(k == DC - 1))
                    for k in range(DC):
                        ins = pe.matmul(dot_ps[par][0:I, S:2 * S], ones[:], xsq[:, par, k, :],
                                        start=(k == 0), stop=(k == DC - 1))
                    ins.then_inc(dots_psum, 1)
                pairs(pe, B, products)

                def gather(b, par, r, again):
                    pe.wait_ge(mask_in[par], (r + 1) * 32)
                    if again:
                        pe.wait_ge(resid_ready, b - 1)
                    for h in range(2):
                        ins = pe.matmul(xt_ps[par][:, h * D:(h + 1) * D], maskb[0:I, par, h * P:(h + 1) * P],
                                        ctxb[0:I, par, :], start=True, stop=True)
                    ins.then_inc(gathered, 1)
                pairs(pe, B, gather)

            @block.scalar
            def _(act):
                rstd_root(act, roots, 1, mv[:, :, 1], rroot[:])

                def transposed(b, par, r, again):
                    act.wait_ge(xnT_psum, b + 1)
                    act.activation(xnT[:, par].rearrange("p c s -> p (c s)"), xt_ps[par], ACT.Copy).then_inc(xnT_ready, 1)
                    act.activation(xsq[:, par].rearrange("p c s -> p (c s)"), xt_ps[par], ACT.Square).then_inc(xnT_ready, 1)
                    act.wait_ge(d2_ready, b + 1)
                    act.activation(root[0:I, par, :], d2[0:I, par, :], ACT.Sqrt).then_inc(root_ready, 1)
                pairs(act, B, transposed)

                act.wait_ge(row_ready, 1)
                act.activation(acc[:, 0, :], row[:, 0, :], ACT.Copy).then_inc(row_saved, 1)
                with act.Fori(0, STEPS // 2) as i:
                    for par in range(2):
                        act.wait_ge(row_ready, 2 * i + par + 2)
                        act.activation(acc[:, 2 * i + par + 1, :], row[:, 1 - par, :], ACT.Copy).then_inc(row_saved, 1)

                def save_marks(n, par):
                    act.wait_ge(mark_ready, n + 1)
                    act.activation(path[:, STEPS - 1 - n, :], marks[:, par, 1:], ACT.Copy).then_inc(mark_saved, 1)
                with act.Fori(0, STEPS // 2) as i:
                    save_marks(2 * i, 0)
                    save_marks(2 * i + 1, 1)

            @block.vector
            def _(dve):
                own = Steps(dve, dve_steps)
                dve.memset(ones[:], 1.0).then_inc(ones_set, 1)
                dve.wait_ge(x_in, 64)
                for t in range(T):
                    own.did(dve.bn_stats(stats[:, t, :], resid[:, t, :]))
                own.seen()
                moments(own, dve, stats, mv, rtmp[:])
                rstd_of(own, dve, roots, 1, mv[:, :, 1], rroot[:], rstd[:], rtmp[:])
                start = own.n

                def normalise(b, par, r, again):
                    if again:
                        dve.wait_ge(xnT_psum, b - 1)
                    for h in range(2):
                        t = 2 * b + h
                        dve.tensor_scalar(xn[:, par, h, :], resid[:, t, :], mv[:, t, 0:1], rstd[:, bass.ds(t, 1)],
                                          ALU.subtract, ALU.mult).then_inc(xn_ready, 1)

                def distances(b, par, rnd, again):
                    own.rounds(start, b, 7)
                    dve.wait_ge(ctx_in[par], (rnd + 1) * 32)
                    dve.tensor_tensor_reduce(csq[0:I, :], ctxb[0:I, par, :], ctxb[0:I, par, :], 1.0, 0.0,
                                             ALU.mult, ALU.add, aa[0:I, par:par + 1]).then_inc(aa_ready, 1)
                    dve.wait_ge(aa_ready, b + 1)
                    dve.wait_ge(dots_psum, b + 1)
                    d, r, s, y = (d2[0:I, par, :], root[0:I, par, :], scr[0:I, 0, :], scr[0:I, 1, :])
                    own.then(dve.tensor_scalar(s, dot_ps[par][0:I, S:2 * S], aa[0:I, par:par + 1], None, ALU.add))
                    own.then(dve.scalar_tensor_tensor(out=s, in0=dot_ps[par][0:I, 0:S], scalar=-2.0, in1=s,
                                                      op0=ALU.mult, op1=ALU.add))
                    dve.tensor_scalar(d, s, 0.0, None, ALU.max).then_inc(d2_ready, 1)
                    dve.wait_ge(d2_ready, b + 1)
                    dve.wait_ge(root_ready, b + 1)
                    own.then(dve.tensor_tensor(s, r, r, ALU.mult))
                    own.did(dve.tensor_tensor(s, d, s, ALU.subtract))
                    own.then(dve.tensor_scalar(y, r, 1e-18, 2.0, ALU.max, ALU.mult))
                    own.then(dve.reciprocal(y, y))
                    own.then(dve.tensor_tensor(s, s, y, ALU.mult))
                    if again:
                        dve.wait_ge(cost_out[par], 16 * rnd)
                    dve.tensor_tensor(dist[0:I, par, :], r, s, ALU.add).then_inc(dist_ready, 1)

                def batch(b, par, r, again):
                    normalise(b, par, r, again)
                    distances(b, par, r, again)
                pairs(dve, B, batch)
                own.rounds(start, B, 7)

                own.did(dve.memset(row[:, 0, 1:], BIG))
                own.did(dve.memset(row[:, 1, :], BIG))
                dve.wait_ge(start_in, 32)
                own.seen()
                dve.sem_inc(row_ready, 1)
                dve.wait_ge(cost_in, 16 * BLK)
                start = own.n

                def forth(s, par, first=False):
                    own.rounds(start, s, 2)
                    old, new = row[:, par], row[:, 1 - par]
                    if not first:
                        dve.wait_ge(row_saved, s)
                    dve.wait_ge(row_ready, s + 1)
                    own.did(dve.tensor_tensor(least[:], old[:, 1:], old[:, 0:BW], ALU.min))
                    own.then(shift_lanes(dve, new[:, 0:1], old[:, BW:BW + 1], 1))
                    dve.tensor_tensor_scan(new[:, 1:], least[:], cost[:, s, :], new[:, 0:1],
                                           ALU.min, ALU.add).then_inc(row_ready, 1)
                forth(0, 0, True)
                forth(1, 1)
                with dve.Fori(1, STEPS // 2) as i:
                    forth(2 * i, 0)
                    forth(2 * i + 1, 1)
                own.rounds(start, STEPS, 2)

                above, diag, lft = acc[:, 0:STEPS, 1:], acc[:, 0:STEPS, 0:BW], acc[:, 1:, 0:BW]
                up_, dg_, lf_ = pick[:, :, 0, :], pick[:, :, 1, :], left[:, :, BW:0:-1]
                dve.wait_ge(row_saved, STEPS + 1)
                own.did(dve.memset(left[:, :, 0:1], 1.0))
                own.then(dve.tensor_tensor(cost[:], above, lft, ALU.min))
                own.did(dve.tensor_tensor(dg_, diag, cost[:], ALU.is_le))
                own.then(dve.tensor_tensor(tie[:], above, lft, ALU.is_le))
                own.then(dve.tensor_tensor(up_, tie[:], dg_, ALU.is_gt))
                own.then(dve.tensor_tensor(lf_, up_, dg_, ALU.is_equal))

                own.did(dve.memset(flow[:], 0.0))
                own.did(dve.memset(marks[:], 0.0))
                own.did(dve.memset(edge[:], 0.0))
                own.seen()
                dve.tensor_tensor_scan(marks[:, 0, ::-1], left[:, STEPS - 1, :], inflow[:, ::-1], edge[:],
                                       ALU.mult, ALU.add).then_inc(mark_ready, 1)
                dve.wait_ge(mark_ready, 1)
                start = own.n

                def back(n, par, s):
                    own.rounds(start, n - 1, 3)
                    old, new = marks[:, 1 - par], marks[:, par]
                    own.did(dve.tensor_tensor(flow[:, :, 1:BW + 1], old[:, 1:].unsqueeze(1).to_broadcast([P, 2, BW]),
                                              pick[:, s + 1, :, :], ALU.mult))
                    own.then(shift_lanes(dve, edge[:], old[:, 0:1], -1))
                    own.then(dve.tensor_tensor(inflow[:], flow[:, 0, 0:BW + 1], flow[:, 1, 1:BW + 2], ALU.add))
                    dve.wait_ge(mark_saved, n)
                    dve.tensor_tensor_scan(new[:, ::-1], left[:, s, :], inflow[:, ::-1], edge[:],
                                           ALU.mult, ALU.add).then_inc(mark_ready, 1)
                    dve.wait_ge(mark_ready, n + 1)
                back(1, 1, STEPS - 2)
                with dve.Fori(1, STEPS // 2) as i:
                    s = dve.snap(STEPS - 1 - 2 * i)
                    back(2 * i, 0, s)
                    back(2 * i + 1, 1, s - 1)

                def add(b, par, r, again):
                    dve.wait_ge(gathered, b + 1)
                    both = resid[:, bass.ds(2 * b, 2), :].rearrange("p h d -> p (h d)")
                    dve.tensor_tensor(both, both, xt_ps[par], ALU.add).then_inc(resid_ready, 1)
                    hold(dve, resid_ready, b + 1)
                    for h in range(2):
                        dve.bn_stats(stats[:, 2 * b + h, :], resid[:, 2 * b + h, :])
                pairs(dve, B, add)


def ffn(nc, psum, resid, mv, stats, ident, roots, w_gateT, w_upT, w_downT):
    KC = INNER // P
    with ExitStack() as c:
        def sb(name, shape, dt=F32):
            return c.enter_context(nc.sbuf_tensor(name, shape, dt))

        def sem(name):
            return c.enter_context(nc.semaphore(name))

        w_f = [sb(f"w{n}_f", [P, DC * INNER]) for n in range(3)]
        w_t = [sb(f"w{n}_t", [P, DC * INNER]) for n in range(3)]
        w_q = [sb(f"w{n}_q", [P, DC * INNER], BF16) for n in range(3)]
        ones = sb("f_ones", [P, P])
        identb = sb("f_identb", [P, P], BF16)
        wabs = sb("wabs", [P, 3])
        wmean = sb("wmean", [P, 3])
        wscale = sb("wscale", [P, 3])
        rstd, rtmp, rroot = sb("f_rstd", [P, T]), sb("f_rtmp", [P, T]), sb("f_rroot", [P, T])
        xn = sb("f_xn", [P, 2, D])
        xr = sb("f_xr", [P, 2, D])
        xq = sb("f_xq", [P, 2, D], BF16)
        xqT = sb("f_xqT", [P, 2, D], BF16)
        amax = sb("f_amax", [P, 2, 1])
        aq = sb("f_aq", [P, 2, 1])
        ad = sb("f_ad", [P, 2, 2])
        silu = sb("f_silu", [P, 2, INNER])
        h = sb("f_h", [P, 2, INNER])
        hr = sb("f_hr", [P, 2, INNER])
        hq = sb("f_hq", [P, 2, INNER], BF16)
        hqT = sb("f_hqT", [P, 2, INNER], BF16)
        magic = sb("f_magic", [P, 1])
        hmax = sb("f_hmax", [P, 2, 1])
        hs = sb("f_hs", [P, 2, 1])
        hd = sb("f_hd", [P, 2, 1])

        w_in = [sem(f"w_in{n}") for n in range(3)]
        setup, w_ones, w_sums, w_ready = sem("f_setup"), sem("w_ones"), sem("w_sums"), sem("w_ready")
        xq_ready, xq_psum, xqT_ready = sem("xq_ready"), sem("xq_psum"), sem("xqT_ready")
        wide_psum, silu_ready, h_ready = sem("wide_psum"), sem("silu_ready"), sem("h_ready")
        hr_ready, hq_ready, hq_psum, hqT_ready = sem("hr_ready"), sem("hq_ready"), sem("hq_psum"), sem("hqT_ready")
        down_psum, resid_new, magic_set = sem("down_psum"), sem("resid_new"), sem("magic_set")
        a_steps, b_steps = sem("f_a_steps"), sem("f_b_steps")

        gate_ps = psum[:, 0:2, :].rearrange("p a n -> p (a n)")
        up_ps = psum[:, 2:4, :].rearrange("p a n -> p (a n)")
        xq_ps = psum[:, 4, :].bitcast(BF16)
        hq_ps = psum[:, 5, :].bitcast(BF16)
        down_ps = [psum[:, 6, 0:D], psum[:, 7, 0:D]]

        with nc.Block() as block:
            @block.sync
            def _(sp):
                sp.dma_start(w_f[0][:].rearrange("p (c n) -> p c n", c=DC), w_gateT.rearrange("(c p) n -> p c n", p=P)).then_inc(w_in[0], 16)
                sp.dma_start(w_f[1][:].rearrange("p (c n) -> p c n", c=DC), w_upT.rearrange("(c p) n -> p c n", p=P)).then_inc(w_in[1], 16)
                sp.dma_start(w_f[2][:].rearrange("p (c n) -> p c n", c=KC), w_downT.rearrange("(c p) n -> p c n", p=P)).then_inc(w_in[2], 16)

            @block.gpsimd
            def _(pool):
                def settle(b, par, r, again):
                    if again:
                        pool.wait_ge(hq_psum, b - 1)
                    pool.wait_ge(hr_ready, b + 1)
                    pool.tensor_tensor(hq[:, par, :], hr[:, par, :], magic[:].to_broadcast([P, INNER]),
                                       ALU.subtract).then_inc(hq_ready, 1)
                pool.memset(magic[:], ROUND).then_inc(magic_set, 1)
                pool.wait_ge(magic_set, 1)
                pairs(pool, T, settle)

            @block.tensor
            def _(pe):
                pe.wait_ge(w_ones, 1)
                pe.wait_ge(setup, 4)
                pe.matmul(psum[:, 7, 0:3], ones[:], wabs[:], start=True, stop=True).then_inc(w_sums, 1)
                pe.wait_ge(w_ready, 3)

                def widen(b, par, r, again):
                    pe.wait_ge(xq_ready, b + 1)
                    for k in range(DC):
                        ins = pe.transpose(xq_ps[:, k * P:(k + 1) * P], xq[:, par, k * P:(k + 1) * P], identb[:])
                    ins.then_inc(xq_psum, 1)
                    pe.wait_ge(xqT_ready, b + 1)
                    if again:
                        pe.wait_ge(h_ready, b)
                    elif par:
                        pe.wait_ge(h_ready, 1)
                    for k in range(DC):
                        for m, bank in ((0, gate_ps), (1, up_ps)):
                            for n in range(INNER // 512):
                                ins = pe.matmul(bank[:, n * 512:(n + 1) * 512], xqT[:, par, k * P:(k + 1) * P],
                                                w_q[m][:, k * INNER + n * 512:k * INNER + (n + 1) * 512],
                                                start=(k == 0), stop=(k == DC - 1))
                    ins.then_inc(wide_psum, 1)

                def narrow(b, par, r, again):
                    pe.wait_ge(hq_ready, b + 1)
                    for k in range(KC):
                        ins = pe.transpose(hq_ps[:, k * P:(k + 1) * P], hq[:, par, k * P:(k + 1) * P], identb[:])
                    ins.then_inc(hq_psum, 1)
                    pe.wait_ge(hqT_ready, b + 1)
                    if again:
                        pe.wait_ge(resid_new, b - 1)
                    for k in range(KC):
                        ins = pe.matmul(down_ps[par], hqT[:, par, k * P:(k + 1) * P], w_q[2][:, k * D:(k + 1) * D],
                                        start=(k == 0), stop=(k == KC - 1))
                    ins.then_inc(down_psum, 1)
                staged(pe, T, (0, widen), (1, narrow))

            @block.scalar
            def _(act):
                rstd_root(act, roots, 2, mv[:, :, 1], rroot[:])

                def first(b, par, r, again):
                    act.wait_ge(xq_psum, b + 1)
                    act.activation(xqT[:, par, :], xq_ps[:, 0:D], ACT.Copy).then_inc(xqT_ready, 1)
                    act.wait_ge(wide_psum, b + 1)
                    act.activation(silu[:, par, :], gate_ps, ACT.Silu, scale=ad[:, par, 0:1]).then_inc(silu_ready, 1)

                def second(b, par, r, again):
                    act.wait_ge(hq_psum, b + 1)
                    act.activation(hqT[:, par, :], hq_ps, ACT.Copy).then_inc(hqT_ready, 1)
                staged(act, T, (0, first), (1, second))

            @block.vector
            def _(dve):
                one, two = Steps(dve, a_steps), Steps(dve, b_steps)
                dve.memset(ones[:], 1.0).then_inc(w_ones, 1)
                dve.tensor_copy(identb[:], ident[:]).then_inc(setup, 1)
                for n in range(3):
                    dve.wait_ge(w_in[n], 16)
                    dve.tensor_reduce(wabs[:, n:n + 1], w_f[n][:], AX.X, ALU.add, apply_absolute_value=True).then_inc(setup, 1)
                moments(one, dve, stats, mv, rtmp[:])
                rstd_of(one, dve, roots, 2, mv[:, :, 1], rroot[:], rstd[:], rtmp[:])
                dve.wait_ge(w_sums, 1)
                one.then(dve.tensor_scalar(wmean[:], psum[:, 7, 0:3], 1.0 / (D * INNER), 1e-5, ALU.mult, ALU.max))
                one.then(dve.reciprocal(wscale[:], wmean[:]))
                for n in range(3):
                    one.then(dve.tensor_scalar(w_t[n][:], w_f[n][:], wscale[:, n:n + 1], ROUND, ALU.mult, ALU.add))
                    one.then(dve.tensor_scalar(w_t[n][:], w_t[n][:], ROUND, -1.0, ALU.subtract, ALU.max))
                    dve.tensor_scalar(w_q[n][:], w_t[n][:], 1.0, None, ALU.min).then_inc(w_ready, 1)
                base = one.n

                def quantise(b, par, r, again):
                    one.rounds(base, b, 6)
                    one.then(dve.tensor_scalar(xn[:, par, :], resid[:, b, :], mv[:, b, 0:1], rstd[:, bass.ds(b, 1)],
                                               ALU.subtract, ALU.mult))
                    one.then(dve.tensor_reduce(amax[:, par, :], xn[:, par, :], AX.X, ALU.max, apply_absolute_value=True))
                    one.then(dve.tensor_scalar(amax[:, par, :], amax[:, par, :], 1e-5, 1.0 / 127.0, ALU.max, ALU.mult))
                    one.did(dve.reciprocal(aq[:, par, :], amax[:, par, :]))
                    if again:
                        dve.wait_ge(silu_ready, b - 1)
                    one.then(dve.tensor_scalar(ad[:, par, :], wmean[:, 0:2], amax[:, par, :], None, ALU.mult))
                    one.then(dve.tensor_scalar(xr[:, par, :], xn[:, par, :], aq[:, par, :], ROUND, ALU.mult, ALU.add))
                    if again:
                        dve.wait_ge(xq_psum, b - 1)
                    dve.tensor_scalar(xq[:, par, :], xr[:, par, :], ROUND, 127.0, ALU.subtract, ALU.min).then_inc(xq_ready, 1)

                def product(b, par, r, again):
                    two.rounds(0, b, 4)
                    dve.wait_ge(silu_ready, b + 1)
                    dve.scalar_tensor_tensor(out=h[:, par, :], in0=up_ps, scalar=ad[:, par, 1:2], in1=silu[:, par, :],
                                             op0=ALU.mult, op1=ALU.mult).then_inc(h_ready, 1)
                    dve.wait_ge(h_ready, b + 1)
                    two.then(dve.tensor_reduce(hmax[:, par, :], h[:, par, :], AX.X, ALU.max, apply_absolute_value=True))
                    two.then(dve.tensor_scalar(hmax[:, par, :], hmax[:, par, :], 1e-5, 1.0 / 127.0, ALU.max, ALU.mult))
                    two.did(dve.reciprocal(hs[:, par, :], hmax[:, par, :]))
                    two.then(dve.tensor_scalar(hd[:, par, :], wmean[:, 2:3], hmax[:, par, :], None, ALU.mult))
                    if again:
                        dve.wait_ge(hq_ready, b - 1)
                    dve.tensor_scalar(hr[:, par, :], h[:, par, :], hs[:, par, :], ROUND, ALU.mult, ALU.add).then_inc(hr_ready, 1)

                def add(b, par, r, again):
                    dve.wait_ge(down_psum, b + 1)
                    dve.scalar_tensor_tensor(out=resid[:, b, :], in0=down_ps[par], scalar=hd[:, par, :], in1=resid[:, b, :],
                                             op0=ALU.mult, op1=ALU.add).then_inc(resid_new, 1)
                    hold(dve, resid_new, b + 1)
                    dve.bn_stats(stats[:, b, :], resid[:, b, :])
                staged(dve, T, (0, quantise), (1, product), (2, add))


def attention(nc, psum, resid, mv, stats, ident, roots, ctxT, wq1, wk1, wv1, wk2, wv2, wo, bo, head_sel_c):
    VW = DH + 1
    PAIRS = HEADS // 2
    UNITS = 3 * PAIRS
    WS = 64.0
    KT = DC + 1
    rows = [P, P, I]
    with ExitStack() as c:
        def sb(name, shape, dt=F32):
            return c.enter_context(nc.sbuf_tensor("t_" + name, shape, dt))

        def sem(name):
            return c.enter_context(nc.semaphore("t_" + name))

        w_f = [sb(f"w_f{n}", [P, DC, HD]) for n in range(5)]
        w_parts = [[sb(f"w_{n}_{part}", [P, DC, HD], F16) for part in "hl"] for n in range(5)]
        wo_sb = sb("wo", [P, HD // P, D])
        bo_sb = sb("bo", [P, 2, D])
        sel_f = sb("sel_f", [2 * HEADS, HEADS * P])
        sel = sb("sel", [2 * HEADS, HEADS * P], BF16)
        identb = sb("identb", [P, P], BF16)
        rstd, rtmp, rroot = sb("rstd", [P, T]), sb("rtmp", [P, T]), sb("rroot", [P, T])
        xn = sb("xn", [P, 2, 2, D])
        xTh, xTl = sb("xTh", [P, DC, S], F16), sb("xTl", [P, DC, S], F16)
        ctxTb = sb("ctxTb", [P, 2, DC, I])
        cTh, cTl = sb("cTh", [P, 2, DC, I], F16), sb("cTl", [P, 2, DC, I], F16)
        qh, ql = [sb(n, [P, 2, HEADS // 2, S], F16) for n in ("qh", "ql")]
        kh, kl = [sb(n, [P, 2, HEADS // 2, KEYS], F16) for n in ("kh", "kl")]
        v = sb("v", [P, 2, KT, HEADS, VW])
        top = sb("top", [P, 2, 2, HEADS])
        shift = sb("shift", [P, 2, 2, 2 * HEADS], BF16)
        shiftT = sb("shiftT", [2 * HEADS, 2, S], BF16)
        probs = sb("probs", [P, 2, 2 * KT, S])
        rsum = sb("rsum", [P, 2, 4])
        o = sb("o", [P, 2, 2, HD])
        oT = sb("oT", [P, HD // P, S])

        w_in, setup, weights_ready = sem("w_in"), sem("setup"), sem("weights_ready")
        ctx_in = [sem(f"ctx_in{n}") for n in range(2)]
        cTh_ready, cTl_ready, biased = sem("cTh_ready"), sem("cTl_ready"), sem("biased")
        own_steps = sem("own_steps")
        xn_ready, xt_psum, xTh_ready, xTl_ready = sem("xn_ready"), sem("xt_psum"), sem("xTh_ready"), sem("xTl_ready")
        q_psum, k_psum, v_psum, qh_ready, kh_ready = sem("q_psum"), sem("k_psum"), sem("v_psum"), sem("qh_ready"), sem("kh_ready")
        bank_free = [sem(f"bank_free{n}") for n in range(2)]
        simA_psum, top_ready, high_ready, shift_ready = sem("simA_psum"), sem("top_ready"), sem("high_ready"), sem("shift_ready")
        shift_psum, shiftT_ready = sem("shift_psum"), sem("shiftT_ready")
        unit_psum, half_psum, exp_ready, pv_psum, rsum_ready, o_ready = (
            sem("unit_psum"), sem("half_psum"), sem("exp_ready"), sem("pv_psum"), sem("rsum_ready"), sem("o_ready"))
        oT_psum, oT_ready, out_psum, added = sem("oT_psum"), sem("oT_ready"), sem("out_psum"), sem("added")

        unit_ps = [psum[:, n, :] for n in range(3)]
        SLOT = [[0, 1, 2], [4, 5, 3]]
        simA_ps = psum[:, 3:5, 0:KEYS]
        pv_ps = psum[:, 5, 0:4 * VW].rearrange("p (g n) -> p g n", n=VW)
        bank = [psum[:, 6, :], psum[:, 7, :]]
        shift_ps = psum[:, 3, :].bitcast(BF16)[0:2 * HEADS, 0:S]

        with nc.Block() as block:
            @block.sync
            def _(sp):
                for dst, src in zip(w_f, (wq1, wk1, wv1, wk2, wv2)):
                    sp.dma_start(dst[:], src.rearrange("(c p) n -> p c n", p=P)).then_inc(w_in, 16)
                sp.dma_start(wo_sb[:], wo.rearrange("(c p) n -> p c n", p=P)).then_inc(w_in, 16)
                for h in range(2):
                    sp.dma_start(bo_sb[:, h, :], bo).then_inc(w_in, 16)
                sp.dma_start(sel_f[:], head_sel_c).then_inc(w_in, 16)

                def load(b, par, r, again):
                    if again:
                        sp.wait_ge(cTl_ready, b - 1)
                    sp.dma_start(ctxTb[:, par], ctxT[b].rearrange("(c p) i -> p c i", p=P)).then_inc(ctx_in[par], 16)
                pairs(sp, B, load)

            @block.gpsimd
            def _(pool):
                pool.wait_ge(w_in, 16 * 9)
                for f, (high, low) in zip(w_f, w_parts):
                    pool.tensor_scalar(high[:], f[:], WS, None, ALU.mult).then_inc(weights_ready, 1)
                for n, (f, (high, low)) in enumerate(zip(w_f, w_parts)):
                    pool.tensor_scalar(f[:], f[:], WS, None, ALU.mult).then_inc(weights_ready, 1)
                for n, (f, (high, low)) in enumerate(zip(w_f, w_parts)):
                    pool.wait_ge(weights_ready, 6 + n)
                    pool.tensor_tensor(low[:], f[:], high[:], ALU.subtract).then_inc(weights_ready, 1)

                def split_context(b, par, r, again):
                    if again:
                        pool.wait_ge(v_psum, KT * (b - 1))
                    pool.wait_ge(cTh_ready, b + 1)
                    pool.tensor_tensor(cTl[:, par], ctxTb[:, par], cTh[:, par], ALU.subtract).then_inc(cTl_ready, 1)
                    pool.wait_ge(xn_ready, 2 * b + 2)
                    pool.tensor_tensor(resid[:, bass.ds(2 * b, 2), :], resid[:, bass.ds(2 * b, 2), :], bo_sb[:],
                                       ALU.add).then_inc(biased, 1)
                pairs(pool, B, split_context)

            @block.tensor
            def _(pe):
                pe.wait_ge(setup, 3)

                def turn(b, par, r, again):
                    pe.wait_ge(xn_ready, 2 * b + 2)
                    if late(b, 1):
                        pe.wait_ge(bank_free[0], 5 * b)
                    if late(b, 3):
                        pe.wait_ge(added, b - 2)
                    for h in range(2):
                        for k in range(DC):
                            ins = pe.transpose(bank[0][:, k * S + h * P:k * S + (h + 1) * P],
                                               xn[:, par, h, k * P:(k + 1) * P], ident[:])
                    ins.then_inc(xt_psum, 1)

                def product(dst, lhs, rhs, last=True):
                    for k in range(DC):
                        for n, (a, c) in enumerate(((0, 0), (0, 1), (1, 0))):
                            ins = pe.matmul(dst, lhs(a, k), rhs(c, k), start=(k == 0 and n == 0), stop=(k == DC - 1 and n == 2))
                    return ins

                def project(b, par, r, again):
                    xT, cT = (xTh, xTl), (cTh, cTl)
                    if not late(b, 1):
                        pe.wait_ge(weights_ready, 15)
                    pe.wait_ge(xTh_ready, b + 1)
                    pe.wait_ge(xTl_ready, b + 1)
                    if late(b, 1):
                        pe.wait_ge(bank_free[1], 5 * b)
                    for n in range(2):
                        if n == 1:
                            pe.wait_ge(bank_free[0], 5 * b + 1)
                        for m in range(2 * n, 2 * n + 2):
                            ins = product(bank[1 - n][:, (m % 2) * S:(m % 2 + 1) * S],
                                          lambda a, k: w_parts[0][a][:, k, m * P:(m + 1) * P], lambda c, k: xT[c][:, k, :])
                        ins.then_inc(q_psum, 1)
                    pe.wait_ge(cTl_ready, b + 1)
                    for m in range(HEADS // 2):
                        g = 1 - m % 2
                        pe.wait_ge(bank_free[g], 5 * b + 1 + (m + 1) // 2)
                        product(bank[g][:, 0:S], lambda a, k: w_parts[1][a][:, k, m * P:(m + 1) * P], lambda c, k: xT[c][:, k, :])
                        product(bank[g][:, S:KEYS], lambda a, k: w_parts[3][a][:, k, m * P:(m + 1) * P],
                                lambda c, k: cT[c][:, par, k, :]).then_inc(k_psum, 1)
                    for j in range(KT):
                        g = 1 - j % 2
                        pe.wait_ge(bank_free[g], 5 * b + 3 + (j + 1) // 2)
                        if j < DC:
                            ins = product(bank[g], lambda a, k: xT[a][:, k, j * P:(j + 1) * P], lambda c, k: w_parts[2][c][:, k, :])
                        else:
                            ins = product(bank[g][0:I, :], lambda a, k: cT[a][:, par, k, :], lambda c, k: w_parts[4][c][:, k, :])
                        ins.then_inc(v_psum, 1)

                def turn_output(b, par, r, again):
                    pe.wait_ge(o_ready, PAIRS * (b + 1))
                    for g in range(2):
                        pe.wait_ge(bank_free[g], 5 * (min(b + 3, B) if isinstance(b, int) else b + 3))
                    for m in range(HD // P):
                        for h in range(2):
                            ins = pe.transpose(bank[m // 2][:, (m % 2) * S + h * P:(m % 2) * S + (h + 1) * P],
                                               o[:, par, h, m * P:(m + 1) * P], ident[:])
                        if m % 2:
                            ins.then_inc(oT_psum, 1)

                def output(b, par, r, again):
                    pe.wait_ge(oT_ready, 2 * b + 2)
                    for h in range(2):
                        for k in range(HD // P):
                            ins = pe.matmul(bank[0][:, h * D:(h + 1) * D], oT[:, k, h * P:(h + 1) * P], wo_sb[:, k, :],
                                            start=(k == 0), stop=(k == HD // P - 1))
                    ins.then_inc(out_psum, 1)

                def scores_for_max(h):
                    lane, m = slice(64 * (h % 2), 64 * (h % 2) + 64), h // 2

                    def body(b, par, r, again):
                        if h == 0:
                            if late(b, 1):
                                pe.wait_ge(shiftT_ready, b)
                            pe.wait_ge(qh_ready, 2 * b + 2)
                            pe.wait_ge(kh_ready, 4 * b + 4)
                        if late(HEADS * b + h, 1):
                            pe.wait_ge(top_ready, HEADS * b + h)
                        for t in range(2):
                            ins = pe.matmul(simA_ps[:, t, :], qh[lane, par, m, t * P:(t + 1) * P], kh[lane, par, m, :],
                                            start=True, stop=True)
                        ins.then_inc(simA_psum, 1)
                    return body

                def score(b, par, h, j):
                    lane, m = slice(64 * (h % 2), 64 * (h % 2) + 64), h // 2
                    slot = SLOT[h % 2][j]
                    dst = unit_ps[slot // 2][0:rows[j], (slot % 2) * S:(slot % 2 + 1) * S]
                    keys = slice(j * P, j * P + rows[j])
                    pe.matmul(dst, sel[:, h * P:h * P + rows[j]], shiftT[:, par, :], start=True, stop=False)
                    pe.matmul(dst, kh[lane, par, m, keys], qh[lane, par, m, :], start=False, stop=False)
                    pe.matmul(dst, kh[lane, par, m, keys], ql[lane, par, m, :], start=False, stop=False)
                    return pe.matmul(dst, kl[lane, par, m, keys], qh[lane, par, m, :], start=False, stop=True)

                def unit_free(b, p, n):
                    if late(UNITS * b + 3 * p + n, 3):
                        pe.wait_ge(exp_ready, UNITS * b + 3 * p + n - 2)

                def scores_first(p):
                    def body(b, par, r, again):
                        if p == 0:
                            pe.wait_ge(bank_free[0], 5 * b + 5)
                            pe.wait_ge(bank_free[1], 5 * b + 5)
                            pe.wait_ge(shiftT_ready, b + 1)
                        unit_free(b, p, 0)
                        score(b, par, 2 * p, 0)
                        score(b, par, 2 * p, 1).then_inc(unit_psum, 1)
                        unit_free(b, p, 1)
                        score(b, par, 2 * p, DC).then_inc(half_psum, 1)
                    return body

                def scores_context(p):
                    def body(b, par, r, again):
                        pe.wait_ge(half_psum, PAIRS * b + p + 1)
                        score(b, par, 2 * p + 1, DC).then_inc(unit_psum, 1)
                    return body

                def scores_second(p):
                    def body(b, par, r, again):
                        unit_free(b, p, 2)
                        score(b, par, 2 * p + 1, 0)
                        score(b, par, 2 * p + 1, 1).then_inc(unit_psum, 1)
                    return body

                def values(p):
                    def body(b, par, r, again):
                        pe.wait_ge(exp_ready, UNITS * b + 3 * p + 3)
                        if late(PAIRS * b + p, 1):
                            pe.wait_ge(o_ready, PAIRS * b + p)
                        for h in (2 * p, 2 * p + 1):
                            for t in range(2):
                                for j in range(KT):
                                    ins = pe.matmul(pv_ps[:, 2 * (h % 2) + t, :],
                                                    probs[0:rows[j], p % 2, SLOT[h % 2][j], t * P:(t + 1) * P],
                                                    v[0:rows[j], par, j, h, :], start=(j == 0), stop=(j == KT - 1))
                        ins.then_inc(pv_psum, 1)
                    return body

                def shifts(b, par, r, again):
                    pe.wait_ge(shift_ready, b + 1)
                    for t in range(2):
                        ins = pe.transpose(shift_ps[:, t * P:(t + 1) * P], shift[:, par, t, :], identb[:])
                    ins.then_inc(shift_psum, 1)

                heads = []
                for p in range(PAIRS):
                    heads += [(0, scores_for_max(2 * p)), (1, scores_first(p))] + [(2, output)] * (p == 2)
                    heads += [(0, scores_for_max(2 * p + 1)), (1, scores_context(p)), (1, scores_second(p))]
                    heads += [(1, values(p - 1))] * (p > 0) + [(2, turn_output)] * (p == 1)
                staged(pe, B, (0, turn), (1, shifts), (2, values(PAIRS - 1)), (0, project), *heads)

            @block.scalar
            def _(act):
                rstd_root(act, roots, 3, mv[:, :, 1], rroot[:])

                def turned(b, par, r, again):
                    if again:
                        act.wait_ge(v_psum, KT * (b - 1))
                    act.wait_ge(ctx_in[par], 16 * (r + 1))
                    act.activation(cTh[:, par], ctxTb[:, par], ACT.Copy).then_inc(cTh_ready, 1)
                    act.wait_ge(xt_psum, b + 1)
                    act.activation(xTh[:].rearrange("p c s -> p (c s)"), bank[0], ACT.Copy).then_inc(xTh_ready, 1)

                def projected(b, par, r, again):
                    for n in range(2):
                        act.wait_ge(q_psum, 2 * b + n + 1)
                        act.activation(qh[:, par, 2 * n:2 * n + 2, :].rearrange("p m s -> p (m s)"), bank[1 - n],
                                       ACT.Copy, scale=1.0 / WS).then_inc(qh_ready, 1)
                    for m in range(HEADS // 2):
                        act.wait_ge(k_psum, 4 * b + m + 1)
                        act.activation(kh[:, par, m, :], bank[1 - m % 2][:, 0:KEYS], ACT.Copy, scale=1.0 / WS).then_inc(kh_ready, 1)
                    if late(b, 2):
                        act.wait_ge(pv_psum, PAIRS * (b - 1))
                    for j in range(KT):
                        act.wait_ge(v_psum, KT * b + j + 1)
                        act.activation(v[0:rows[j], par, j, :, 0:DH],
                                       bank[1 - j % 2][0:rows[j], :].rearrange("p (h d) -> p h d", d=DH),
                                       ACT.Copy, scale=1.0 / WS).then_inc(bank_free[1 - j % 2], 1)

                def turned_output(b, par, r, again):
                    for n in range(2):
                        act.wait_ge(oT_psum, 2 * b + n + 1)
                        act.activation(oT[:, 2 * n:2 * n + 2, :].rearrange("p m s -> p (m s)"), bank[n], ACT.Copy).then_inc(oT_ready, 1)

                def exponentials(p):
                    def body(b, par, r, again):
                        for n in range(3):
                            act.wait_ge(unit_psum, UNITS * b + 3 * p + n + 1)
                            if n == 0 and late(PAIRS * b + p, 2):
                                act.wait_ge(pv_psum, PAIRS * b + p - 1)
                            top_row = I if n == 1 else P
                            act.activation(probs[0:top_row, p % 2, 2 * n:2 * n + 2, :].rearrange("p j s -> p (j s)"),
                                           unit_ps[n][0:top_row, :], ACT.Exp, scale=DH ** -0.5).then_inc(exp_ready, 1)
                    return body

                def shifted(b, par, r, again):
                    act.wait_ge(shift_psum, b + 1)
                    act.activation(shiftT[:, par, :], shift_ps, ACT.Copy).then_inc(shiftT_ready, 1)
                exps = [(1, exponentials(p)) for p in range(PAIRS)]
                staged(act, B, (0, turned), (1, shifted), (0, projected), *exps[:2], (2, turned_output), *exps[2:])

            @block.vector
            def _(dve):
                own = Steps(dve, own_steps)
                dve.memset(v[:, :, :, :, DH:VW], 1.0).then_inc(setup, 1)
                dve.tensor_copy(identb[:], ident[:]).then_inc(setup, 1)
                moments(own, dve, stats, mv, rtmp[:])
                rstd_of(own, dve, roots, 3, mv[:, :, 1], rroot[:], rstd[:], rtmp[:])
                dve.wait_ge(w_in, 16 * 9)
                dve.tensor_copy(sel[:], sel_f[:]).then_inc(setup, 1)

                def normalise(b, par, r, again):
                    if again:
                        dve.wait_ge(xt_psum, b - 1)
                    for h in range(2):
                        dve.tensor_scalar(xn[:, par, h, :], resid[:, 2 * b + h, :], mv[:, 2 * b + h, 0:1],
                                          rstd[:, bass.ds(2 * b + h, 1)], ALU.subtract, ALU.mult).then_inc(xn_ready, 1)

                def less(out, psum_of, high):
                    return dve.scalar_tensor_tensor(out=out, in0=psum_of, scalar=1.0 / WS, in1=high, op0=ALU.mult, op1=ALU.subtract)

                def low_x(b, par, r, again):
                    dve.wait_ge(xTh_ready, b + 1)
                    flat = [x[:].rearrange("p c s -> p (c s)") for x in (xTh, xTl)]
                    dve.tensor_tensor(flat[1], bank[0], flat[0], ALU.subtract).then_inc(xTl_ready, 1)
                    dve.wait_ge(xTl_ready, b + 1)
                    dve.sem_inc(bank_free[0], 1)

                def lows(b, par, r, again):
                    for n in range(2):
                        dve.wait_ge(qh_ready, 2 * b + n + 1)
                        flat = [x[:, par, 2 * n:2 * n + 2, :].rearrange("p m s -> p (m s)") for x in (qh, ql)]
                        less(flat[1], bank[1 - n], flat[0]).then_inc(bank_free[1 - n], 1)
                    for m in range(HEADS // 2):
                        dve.wait_ge(kh_ready, 4 * b + m + 1)
                        less(kl[:, par, m, :], bank[1 - m % 2][:, 0:KEYS], kh[:, par, m, :]).then_inc(bank_free[1 - m % 2], 1)

                def maxima(h):
                    def body(b, par, r, again):
                        dve.wait_ge(simA_psum, HEADS * b + h + 1)
                        dve.tensor_reduce(top[:, par, :, h], simA_ps, AX.X, ALU.max).then_inc(top_ready, 1)
                    return body

                def split(b, par, r, again):
                    dve.wait_ge(top_ready, HEADS * (b + 1))
                    if late(b, 2):
                        dve.wait_ge(shift_psum, b - 1)
                    dve.tensor_scalar(shift[:, par, :, 0:HEADS], top[:, par], -1.0, None, ALU.mult).then_inc(high_ready, 1)
                    dve.wait_ge(high_ready, b + 1)
                    dve.scalar_tensor_tensor(out=shift[:, par, :, HEADS:], in0=top[:, par], scalar=-1.0,
                                             in1=shift[:, par, :, 0:HEADS], op0=ALU.mult, op1=ALU.subtract).then_inc(shift_ready, 1)

                def normal(p):
                    def body(b, par, r, again):
                        dve.wait_ge(pv_psum, PAIRS * b + p + 1)
                        dve.reciprocal(rsum[:, p % 2, :], pv_ps[:, :, DH]).then_inc(rsum_ready, 1)
                        if p == 0 and late(b, 2):
                            dve.wait_ge(oT_psum, 2 * (b - 1))
                        dve.wait_ge(rsum_ready, PAIRS * b + p + 1)
                        for u in range(2):
                            ins = dve.tensor_tensor(o[:, par, :, (2 * p + u) * DH:(2 * p + u + 1) * DH],
                                                    pv_ps[:, 2 * u:2 * u + 2, 0:DH],
                                                    rsum[:, p % 2, 2 * u:2 * u + 2].unsqueeze(2).to_broadcast([P, 2, DH]), ALU.mult)
                        ins.then_inc(o_ready, 1)
                    return body

                def add(b, par, r, again):
                    dve.wait_ge(biased, b + 1)
                    dve.wait_ge(out_psum, b + 1)
                    both = resid[:, bass.ds(2 * b, 2), :].rearrange("p h d -> p (h d)")
                    dve.tensor_tensor(both, both, bank[0], ALU.add).then_inc(added, 1)
                    hold(dve, added, b + 1)
                    for h in range(2):
                        dve.bn_stats(stats[:, 2 * b + h, :], resid[:, 2 * b + h, :])

                heads = []
                for p in range(PAIRS):
                    heads += [(1, maxima(2 * p)), (1, maxima(2 * p + 1))] + [(0, normalise)] * (p == 0) + [(3, add)] * (p == 2)
                    heads += [(2, normal(p - 1))] * (p > 0)
                staged(dve, B, (1, low_x), (3, normal(PAIRS - 1)), (1, lows), *heads, (1, split))


def moe(nc, psum, resid, mv, stats, ident, roots, phiT, phi_b, expert_w, expert_b, consts, out):
    PHI = 64.0
    Q = 4
    QS = SLOTS // Q
    QE = NE // Q
    ST = SLOTS // P
    EP = P // PS
    G = 8
    GT = T // G
    GW = GT * P
    with ExitStack() as outer:
        def sb(name, shape, dt=F32):
            return outer.enter_context(nc.sbuf_tensor("m_" + name, shape, dt))

        def sem(name):
            return outer.enter_context(nc.semaphore("m_" + name))
        xTh, xTl = sb("xTh", [P, DC, T * P], F16), sb("xTl", [P, DC, T * P], F16)
        ph, pl = sb("ph", [P, DC, SLOTS], F16), sb("pl", [P, DC, SLOTS], F16)
        shiftC = sb("shiftC", [2 * PS, T * P], BF16)
        phib_col = sb("phib_col", [P, ST])
        yh, yl = sb("yh", [P, ST, D], F16), sb("yl", [P, ST, D], F16)
        gather_slots(nc, psum, resid, mv, stats, ident, roots, phiT, phi_b, expert_w, expert_b, consts,
                     xTh, xTl, ph, pl, shiftC, phib_col, yh, yl, PHI, Q, QS, QE, ST, EP)
        selC_f = sb("selC_f", [2 * PS, P])
        selC = sb("selC", [2 * PS, P], BF16)
        sel_sum = sb("sel_sum", [P, P])
        e = sb("e", [P, 2, ST, GW])
        total = sb("total", [P, 2, GW])
        inv = sb("inv", [P, 2, GW])
        ch, cl = sb("ch", [P, 4, GW], F16), sb("cl", [P, 4, GW], F16)
        c_in, selC_ready = sem("c_in"), sem("selC_ready")
        lt_psum, ex_ready, tot_ready, sum_psum, inv_ready = (
            sem("lt_psum"), sem("ex_ready"), sem("tot_ready"), sem("sum_psum"), sem("inv_ready"))
        norm_ready, ch_ready, cl_ready, y_step, y_psum, y_added, stored = (
            sem("norm_ready"), sem("ch_ready"), sem("cl_ready"), sem("y_step"), sem("y_psum"), sem("y_added"), sem("stored"))
        LT = 3
        lt_ps = [psum[:, n, :] for n in range(LT)]
        sum_ps = psum[:, LT, :]
        y_ps = psum[:, LT + 1:8, :].rearrange("p (g a) (t d) -> p g (a t) d", g=2, d=D)

        def behind(by, at, step):
            return (1, step(at - by)) if at >= by else (2, step(ST + at - by))

        with nc.Block() as block:
            @block.sync
            def _(sp):
                sp.dma_start(selC_f[:], consts["selC"]).then_inc(c_in, 16)
                sp.dma_start(sel_sum[:], consts["sel_sum"]).then_inc(c_in, 16)
                rows = out.rearrange("b (h p) d -> p (b h) d", p=P)

                def store(b, par, r, again):
                    sp.wait_ge(y_added, 2 * b + 2)
                    sp.dma_start(rows[:, bass.ds(GT * b, GT), :], resid[:, bass.ds(GT * b, GT), :]).then_inc(stored, 16)
                pairs(sp, G, store)
                sp.wait_ge(stored, 16 * G)

            @block.tensor
            def _(pe):
                pe.wait_ge(c_in, 32)
                pe.wait_ge(selC_ready, 1)

                def logits(s):
                    def body(b, par, r, again):
                        if late(ST * b + s, LT):
                            pe.wait_ge(ex_ready, ST * b + s - LT + (2 if par == 0 and s < 2 else 1))
                        dst, slots, toks = lt_ps[(ST * par + s) % LT], slice(s * P, (s + 1) * P), bass.ds(GW * b, GW)
                        for k in range(DC):
                            pe.matmul(dst, ph[:, k, slots], xTh[:, k, toks], start=(k == 0), stop=False)
                            pe.matmul(dst, ph[:, k, slots], xTl[:, k, toks], start=False, stop=False)
                            pe.matmul(dst, pl[:, k, slots], xTh[:, k, toks], start=False, stop=False)
                        pe.matmul(dst, selC[:], shiftC[:, toks], start=False, stop=True).then_inc(lt_psum, 1)
                    return body

                def spread(s):
                    def body(b, par, r, again):
                        pe.wait_ge(cl_ready, ST * b + s + 1)
                        if s == 0 and late(b, 2):
                            pe.wait_ge(y_added, 2 * b - 2)
                        for t in range(GT):
                            toks = slice(t * P, (t + 1) * P)
                            pe.matmul(y_ps[:, par, t, :], ch[:, s % 4, toks], yh[:, s, :], start=(s == 0 and t % 2 == 0),
                                      stop=False, skip_group_check=True)
                            pe.matmul(y_ps[:, par, t, :], ch[:, s % 4, toks], yl[:, s, :], start=False, stop=False, skip_group_check=True)
                            ins = pe.matmul(y_ps[:, par, t, :], cl[:, s % 4, toks], yh[:, s, :], start=False, stop=(s == ST - 1),
                                            skip_group_check=True)
                        ins.then_inc(y_step, 1)
                    return body

                def sums(b, par, r, again):
                    pe.wait_ge(tot_ready, ST * b + ST)
                    if late(b, 1):
                        pe.wait_ge(inv_ready, b)
                    pe.matmul(sum_ps, sel_sum[:], total[:, (ST - 1) % 2, :], start=True, stop=True).then_inc(sum_psum, 1)
                steps = []
                for s in range(ST):
                    steps += [(0, logits(s))] + [(1, sums)] * (s == 1) + [behind(4, s, spread)]
                staged(pe, G, *steps)

            @block.scalar
            def _(act):
                def exponential(s):
                    def body(b, par, r, again):
                        act.wait_ge(lt_psum, ST * b + s + 1)
                        if late(b, 2):
                            act.wait_ge(cl_ready, ST * (b - 2) + s + 1)
                        act.activation(e[:, par, s, :], lt_ps[(ST * par + s) % LT], ACT.Exp, bias=phib_col[:, s:s + 1],
                                       scale=1.0 / PHI).then_inc(ex_ready, 1)
                    return body

                def high(s):
                    def body(b, par, r, again):
                        act.wait_ge(norm_ready, ST * b + s + 1)
                        if late(ST * b + s, 4):
                            act.wait_ge(y_step, ST * b + s - 3)
                        act.activation(ch[:, s % 4, :], e[:, par, s, :], ACT.Copy).then_inc(ch_ready, 1)
                    return body
                steps = []
                for s in range(ST):
                    steps += [behind(3, s, high), (0, exponential(s))]
                staged(act, G, *steps)

            @block.gpsimd
            def _(pool):
                def low(s):
                    def body(b, par, r, again):
                        pool.wait_ge(ch_ready, ST * b + s + 1)
                        pool.tensor_tensor(cl[:, s % 4, :], e[:, par, s, :], ch[:, s % 4, :], ALU.subtract).then_inc(cl_ready, 1)
                    return body
                staged(pool, G, *[(0, low(s)) for s in range(ST)])

            @block.vector
            def _(dve):
                dve.wait_ge(c_in, 32)
                dve.tensor_copy(selC[:], selC_f[:]).then_inc(selC_ready, 1)

                def accumulate(s):
                    def body(b, par, r, again):
                        if s == 0:
                            return
                        dve.wait_ge(ex_ready, ST * b + s + 1)
                        before = e[:, par, 0, :] if s == 1 else total[:, (s - 1) % 2, :]
                        if s > 1:
                            dve.wait_ge(tot_ready, ST * b + s)
                        if s == 1 and late(b, 1):
                            dve.wait_ge(sum_psum, b)
                        ins = dve.tensor_tensor(total[:, s % 2, :], before, e[:, par, s, :], ALU.add)
                        ins.then_inc(tot_ready, 2 if s == 1 else 1)
                    return body

                def normalise(s):
                    def body(b, par, r, again):
                        if s == 0:
                            dve.wait_ge(inv_ready, b + 1)
                        dve.tensor_tensor(e[:, par, s, :], e[:, par, s, :], inv[:, par, :], ALU.mult).then_inc(norm_ready, 1)
                    return body

                def invert(b, par, r, again):
                    dve.wait_ge(sum_psum, b + 1)
                    dve.reciprocal(inv[:, par, :], sum_ps).then_inc(inv_ready, 1)

                def add(b, par, r, again):
                    dve.wait_ge(y_step, ST * (b + 1))
                    for t in range(2):
                        both = resid[:, bass.ds(GT * b + 2 * t, 2), :]
                        dve.tensor_tensor(both, both, y_ps[:, par, 2 * t:2 * t + 2, :], ALU.add).then_inc(y_added, 1)
                steps = []
                for s in range(ST):
                    steps += [(0, accumulate(s))] + [(1, invert)] * (s == 1) + [behind(2, s, normalise)] + [(2, add)] * (s == 4)
                staged(dve, G, *steps)


def gather_slots(nc, psum, resid, mv, stats, ident, roots, phiT, phi_b, expert_w, expert_b, consts,
                 xTh, xTl, ph, pl, shiftC, phib_col, yh, yl, PHI, Q, QS, QE, ST, EP):
    with ExitStack() as c:
        def sb(name, shape, dt=F32):
            return c.enter_context(nc.sbuf_tensor("g_" + name, shape, dt))

        def sem(name):
            return c.enter_context(nc.semaphore("g_" + name))
        slots_in = sb("slots_in", [P, DC, SLOTS])
        cmax = sb("cmax", [P, T, Q, PS])
        with ExitStack() as c1:
            def sb1(name, shape, dt=F32):
                return c1.enter_context(nc.sbuf_tensor("g_" + name, shape, dt))
            xh, xl = sb1("xh", [P, T, D], F16), sb1("xl", [P, T, D], F16)
            identb = sb1("identb", [P, P], BF16)
            rstd, rtmp, rroot = sb1("rstd", [P, T]), sb1("rtmp", [P, T]), sb1("rroot", [P, T])
            xn = sb1("xn", [P, 2, D])
            pb_row = cmax[0:1].rearrange("p t q s -> p (t q s)")[:, 0:SLOTS]
            pb_parts = [x[0:1].rearrange("p s d -> p (s d)").bitcast(BF16)[:, a:a + SLOTS]
                        for x, a in ((yh, 0), (yh, SLOTS), (yl, 0))]
            pb3 = sb1("pb3", [3, SLOTS], BF16)
            ones3 = sb1("ones3", [3, P], BF16)
            selD_f = sb1("selD_f", [2 * QE, QS])
            selD = sb1("selD", [2 * QE, QS], BF16)
            top = sb1("top", [P, 2, QE])
            sp_ = sb1("sp", [P, 2, 2 * QE], BF16)
            spT = sb1("spT", [2 * QE, 2, P], BF16)
            e = sb1("e", [P, 4, QS])
            esum, einv = sb1("esum", [P, 2, QE]), sb1("einv", [P, 2, QE])
            dh, dl = sb1("dh", [P, 4, QS], F16), sb1("dl", [P, 4, QS], F16)
            phi_f = slots_in

            w_in, parts_in, setup = sem("w_in"), sem("parts_in"), sem("setup")
            own_steps, phi_ready, parts_ready = (
                sem("own_steps"), sem("phi_ready"), sem("parts_ready"))
            xn_ready, xh_ready, x_psum, xTh_ready, xl_ready, xTl_ready = (
                sem("xn_ready"), sem("xh_ready"), sem("x_psum"), sem("xTh_ready"), sem("xl_ready"), sem("xTl_ready"))
            log_psum, top_ready, hi_ready, sp_ready, spT_psum, spT_ready, shift_psum = (
                sem("log_psum"), sem("top_ready"), sem("hi_ready"), sem("sp_ready"), sem("spT_psum"), sem("spT_ready"), sem("shift_psum"))
            ex_ready, esum_ready, einv_ready, dn_ready, dh_ready, dl_ready, slot_psum, slot_taken = (
                sem("ex_ready"), sem("esum_ready"), sem("einv_ready"), sem("dn_ready"), sem("dh_ready"), sem("dl_ready"),
                sem("slot_psum"), sem("slot_taken"))
            x_ps = [psum[:, n, 0:D] for n in range(2)]
            log_ps = [psum[:, n, :] for n in range(4)]
            spT_ps = psum[:, 4, :].bitcast(BF16)
            slot_ps = [psum[:, 5, :], psum[:, 6, :]]

            with nc.Block() as block:
                @block.sync
                def _(sp):
                    sp.dma_start(phi_f[:], phiT.rearrange("(c p) n -> p c n", p=P)).then_inc(w_in, 16)
                    sp.dma_start(pb_row, phi_b).then_inc(w_in, 16)
                    sp.dma_start(selD_f[:], consts["selD"]).then_inc(w_in, 16)
                    sp.dma_start(phib_col[:], consts["phi_b_col"]).then_inc(w_in, 16)
                    sp.wait_ge(parts_ready, 3)
                    for n in range(3):
                        sp.dma_start(pb3[n:n + 1, :], pb_parts[n]).then_inc(parts_in, 16)

                @block.tensor
                def _(pe):
                    def turn(b, par, r, again):
                        pe.wait_ge(xn_ready, b + 1)
                        if again:
                            pe.wait_ge(xTl_ready, b - 1)
                        for k in range(DC):
                            ins = pe.transpose(x_ps[par][:, k * P:(k + 1) * P], xn[:, par, k * P:(k + 1) * P], ident[:])
                        ins.then_inc(x_psum, 1)
                    pairs(pe, T, turn)
                    pe.wait_ge(xTl_ready, T)
                    pe.wait_ge(setup, 3)
                    pe.wait_ge(phi_ready, 2)
                    pe.wait_ge(parts_in, 48)

                    with pe.Fori(0, Q) as q:
                        def logits(t, slot, r, again):
                            u = T * q + t
                            if late(t, 4):
                                pe.wait_ge(ex_ready, u - 3)
                            dst, toks, cols = log_ps[slot], bass.ds(t * P, P), bass.ds(q * QS, QS)
                            for k in range(DC):
                                pe.matmul(dst, xTh[:, k, toks], ph[:, k, cols], start=(k == 0), stop=False)
                                pe.matmul(dst, xTh[:, k, toks], pl[:, k, cols], start=False, stop=False)
                                pe.matmul(dst, xTl[:, k, toks], ph[:, k, cols], start=False, stop=False)
                            pe.matmul(dst, ones3[:], pb3[:, cols], start=False, stop=True).then_inc(log_psum, 1)

                        def turn_tops(t, slot, r, again):
                            u = T * q + t
                            pe.wait_ge(sp_ready, u + 1)
                            if late(t, 1):
                                pe.wait_ge(spT_ready, u)
                            pe.transpose(spT_ps[0:2 * QE, 0:P], sp_[:, slot % 2, :], identb[:]).then_inc(spT_psum, 1)

                        def gather(t, slot, r, again):
                            u = T * q + t
                            pe.wait_ge(dl_ready, u + 1)
                            if not late(t, 1):
                                pe.wait_ge(slot_taken, 2 * q + 1)
                            first, last = isinstance(t, int) and t == 0, isinstance(t, int) and t == T - 1
                            for k in range(DC):
                                high = xh[:, t, k * P:(k + 1) * P]
                                pe.matmul(slot_ps[k], high, dh[:, slot, :], start=first, stop=False, skip_group_check=True)
                                pe.matmul(slot_ps[k], high, dl[:, slot, :], start=False, stop=False, skip_group_check=True)
                                ins = pe.matmul(slot_ps[k], xl[:, t, k * P:(k + 1) * P], dh[:, slot, :], start=False, stop=last,
                                                skip_group_check=True)
                            ins.then_inc(slot_psum, 1)

                        def shift(t, slot, r, again):
                            pe.wait_ge(spT_ready, T * q + t + 1)
                            pe.matmul(log_ps[slot], spT[:, slot % 2, :], selD[:], start=False, stop=True,
                                      skip_group_check=True).then_inc(shift_psum, 1)
                        staged(pe, T, (0, logits), (1, turn_tops), (4, gather), (1, shift), unroll=4)

                @block.scalar
                def _(act):
                    rstd_root(act, roots, 4, mv[:, :, 1], rroot[:])

                    def highs(b, par, r, again):
                        hold(act, xn_ready, b + 1)
                        act.activation(xh[:, b, :], xn[:, par, :], ACT.Copy).then_inc(xh_ready, 1)
                        hold(act, x_psum, b + 1)
                        act.activation(xTh[:, :, bass.ds(b * P, P)], x_ps[par].rearrange("p (c t) -> p c t", c=DC),
                                       ACT.Copy).then_inc(xTh_ready, 1)
                    pairs(act, T, highs)

                    with act.Fori(0, Q) as q:
                        def take_tops(t, slot, r, again):
                            act.wait_ge(spT_psum, T * q + t + 1)
                            act.activation(spT[:, slot % 2, :], spT_ps[0:2 * QE, 0:P], ACT.Copy).then_inc(spT_ready, 1)

                        def exponential(t, slot, r, again):
                            u = T * q + t
                            act.wait_ge(shift_psum, u + 1)
                            if late(t, 4):
                                act.wait_ge(dl_ready, u - 3)
                            act.activation(e[:, slot, :], log_ps[slot], ACT.Exp, scale=1.0 / PHI).then_inc(ex_ready, 1)

                        def high(t, slot, r, again):
                            u = T * q + t
                            act.wait_ge(dn_ready, u + 1)
                            if late(t, 4):
                                act.wait_ge(slot_psum, u - 3)
                            act.activation(dh[:, slot, :], e[:, slot, :], ACT.Copy).then_inc(dh_ready, 1)
                        staged(act, T, (0, take_tops), (0, exponential), (1, high), unroll=4)

                @block.gpsimd
                def _(pool):
                    with pool.Fori(0, Q) as q:
                        def product(t, slot, r, again):
                            u = T * q + t
                            pool.wait_ge(einv_ready, u + 1)
                            pool.tensor_tensor(e[:, slot, :].rearrange("p (n s) -> p n s", s=PS),
                                               e[:, slot, :].rearrange("p (n s) -> p n s", s=PS),
                                               einv[:, slot % 2, :].unsqueeze(2).to_broadcast([P, QE, PS]),
                                               ALU.mult).then_inc(dn_ready, 1)

                        def low(t, slot, r, again):
                            pool.wait_ge(dh_ready, T * q + t + 1)
                            pool.tensor_tensor(dl[:, slot, :], e[:, slot, :], dh[:, slot, :], ALU.subtract).then_inc(dl_ready, 1)
                        staged(pool, T, (0, product), (1, low), unroll=4)

                @block.vector
                def _(dve):
                    own = Steps(dve, own_steps)
                    dve.sem_inc(slot_taken, 1)
                    dve.memset(ones3[:], 1.0).then_inc(setup, 1)
                    dve.tensor_copy(identb[:], ident[:]).then_inc(setup, 1)
                    moments(own, dve, stats, mv, rtmp[:])
                    rstd_of(own, dve, roots, 4, mv[:, :, 1], rroot[:], rstd[:], rtmp[:])

                    def parts(b, par, r, again):
                        if late(b, 2):
                            dve.wait_ge(xh_ready, b - 1)
                            dve.wait_ge(x_psum, b - 1)
                            dve.wait_ge(xl_ready, b - 1)
                        dve.tensor_scalar(xn[:, par, :], resid[:, b, :], mv[:, b, 0:1], rstd[:, bass.ds(b, 1)],
                                          ALU.subtract, ALU.mult).then_inc(xn_ready, 1)

                    def lows(b, par, r, again):
                        dve.wait_ge(xh_ready, b + 1)
                        dve.tensor_tensor(xl[:, b, :], xn[:, par, :], xh[:, b, :], ALU.subtract).then_inc(xl_ready, 1)
                        dve.wait_ge(xTh_ready, b + 1)
                        toks = bass.ds(b * P, P)
                        dve.tensor_tensor(xTl[:, :, toks], x_ps[par].rearrange("p (c t) -> p c t", c=DC), xTh[:, :, toks],
                                          ALU.subtract).then_inc(xTl_ready, 1)
                    staged(dve, T, (0, parts), (1, lows))

                    dve.wait_ge(w_in, 64)
                    dve.tensor_copy(selD[:], selD_f[:]).then_inc(setup, 1)
                    for k in range(DC):
                        own.then(dve.tensor_scalar(ph[:, k, :], phi_f[:, k, :], PHI, None, ALU.mult))
                        dve.scalar_tensor_tensor(out=pl[:, k, :], in0=phi_f[:, k, :], scalar=PHI, in1=ph[:, k, :],
                                                 op0=ALU.mult, op1=ALU.subtract).then_inc(phi_ready, 1)
                    own.then(dve.tensor_scalar(pb_row, pb_row, PHI, None, ALU.mult))
                    for n in range(3):
                        dve.tensor_copy(pb_parts[n], pb_row).then_inc(parts_ready, 1)
                        if n < 2:
                            dve.wait_ge(parts_ready, n + 1)
                            own.then(dve.tensor_tensor(pb_row, pb_row, pb_parts[n], ALU.subtract))
                    dve.wait_ge(phi_ready, 2)

                    with dve.Fori(0, Q) as q:
                        def tops(t, slot, r, again):
                            u = T * q + t
                            par = slot % 2
                            dve.wait_ge(log_psum, u + 1)
                            dve.tensor_reduce(top[:, par, :], log_ps[slot].rearrange("p (n s) -> p n s", s=PS),
                                              AX.X, ALU.max).then_inc(top_ready, 1)
                            dve.tensor_reduce(cmax[:, t, q, :], log_ps[slot].rearrange("p (n s) -> p s n", s=PS),
                                              AX.X, ALU.max)
                            dve.wait_ge(top_ready, u + 1)
                            if late(t, 2):
                                dve.wait_ge(spT_psum, u - 1)
                            dve.tensor_scalar(sp_[:, par, 0:QE], top[:, par, :], -1.0, None, ALU.mult).then_inc(hi_ready, 1)
                            dve.wait_ge(hi_ready, u + 1)
                            dve.scalar_tensor_tensor(out=sp_[:, par, QE:], in0=top[:, par, :], scalar=-1.0,
                                                     in1=sp_[:, par, 0:QE], op0=ALU.mult, op1=ALU.subtract).then_inc(sp_ready, 1)

                        def sums(t, slot, r, again):
                            u = T * q + t
                            par = slot % 2
                            dve.wait_ge(ex_ready, u + 1)
                            dve.tensor_reduce(esum[:, par, :], e[:, slot, :].rearrange("p (n s) -> p n s", s=PS),
                                              AX.X, ALU.add).then_inc(esum_ready, 1)
                            dve.wait_ge(esum_ready, u + 1)
                            if late(t, 2):
                                dve.wait_ge(dn_ready, u - 1)
                            dve.reciprocal(einv[:, par, :], esum[:, par, :]).then_inc(einv_ready, 1)
                        staged(dve, T, (0, tops), (1, sums), unroll=4)
                        for k in range(DC):
                            dve.wait_ge(slot_psum, T * (q + 1))
                            dve.tensor_copy(slots_in[:, k, bass.ds(q * QS, QS)], slot_ps[k]).then_inc(slot_taken, 1)

        experts(nc, psum, ident, roots, slots_in, cmax, expert_w, expert_b, consts, shiftC, yh, yl, Q, ST, EP)


def experts(nc, psum, ident, roots, slots_in, cmax, expert_w, expert_b, consts, shiftC, yh, yl, Q, ST, EP):
    RING = 4
    with ExitStack() as c:
        def sb(name, shape, dt=F32):
            return c.enter_context(nc.sbuf_tensor("x_" + name, shape, dt))

        def sem(name):
            return c.enter_context(nc.semaphore("x_" + name))
        w = sb("w", [P, RING, EP, DC, D])
        bias = sb("bias", [EP, RING, D])
        esel = sb("esel", [EP, P])
        identb = sb("identb", [P, P], BF16)
        xT = sb("xT", [P, 2, DC, P])
        slots = sb("slots", [P, ST, D])
        smv, sstats = sb("smv", [P, ST, 2]), sb("sstats", [P, ST, 6])
        rstd, rtmp, rroot = sb("rstd", [P, ST]), sb("rtmp", [P, ST]), sb("rroot", [P, ST])
        a = sb("a", [P, 2, D])
        th = sb("th", [P, 2, D])
        thT = sb("thT", [P, 2, D])
        y = sb("y", [P, 2, D])
        cm = sb("cm", [P, T, PS])
        cs2 = cmax[:].rearrange("p t q s -> p (t q s)")[:, 0:T * PS].bitcast(BF16).rearrange("p (t u s) -> p t u s", u=2, s=2 * PS)
        cs = cs2.rearrange("p t u s -> p (t u) s")
        w_in = [sem(f"w_in{n}") for n in range(RING)]
        b_in, setup, own_steps = sem("b_in"), sem("setup"), sem("own_steps")
        copied, slot_psum, clipped, cs_ready, cs_psum, cs_taken = (
            sem("copied"), sem("slot_psum"), sem("clipped"), sem("cs_ready"), sem("cs_psum"), sem("cs_taken"))
        a_ready, th_ready, th_psum, thT_ready, y_psum, y_ready, yh_ready, yl_ready = (
            sem("a_ready"), sem("th_ready"), sem("th_psum"), sem("thT_ready"), sem("y_psum"), sem("y_ready"), sem("yh_ready"), sem("yl_ready"))
        bank = [psum[:, n, 0:D] for n in range(8)]

        with nc.Block() as block:
            @block.sync
            def _(sp):
                sp.dma_start(esel[:], consts["esel"]).then_inc(b_in, 16)

                def load(s, slot, r, again):
                    if late(s, RING):
                        sp.wait_ge(y_psum, s - RING + 1)
                    sp.dma_start(bias[:, slot, :], expert_b[bass.ds(EP * s, EP), :]).then_inc(w_in[slot], 16)
                    for j in range(EP):
                        sp.dma_start(w[:, slot, j], expert_w[EP * s + j].rearrange("(c p) n -> p c n", p=P)).then_inc(w_in[slot], 16)
                staged(sp, ST, (0, load), unroll=RING)

            @block.tensor
            def _(pe):
                pe.wait_ge(setup, 1)

                def turn(s, par, r, again):
                    pe.wait_ge(copied, s + 1)
                    if again:
                        pe.wait_ge(clipped, s - 1)
                    for k in range(DC):
                        ins = pe.transpose(bank[par][:, k * P:(k + 1) * P], xT[:, par, k, :], ident[:])
                    ins.then_inc(slot_psum, 1)
                pairs(pe, ST, turn)
                pe.wait_ge(cs_ready, 1)

                def turn_max(t, par, r, again):
                    if again:
                        pe.wait_ge(cs_taken, 2 * t - 2)
                    pe.transpose(psum[:, 2 + par, :].bitcast(BF16)[:, 0:P],
                                 cs2[:, t].rearrange("p t s -> p (t s)"), identb[:]).then_inc(cs_psum, 1)
                pairs(pe, T // 2, turn_max)
                pe.wait_ge(b_in, 16)

                def run(s, slot, r, again):
                    par = slot % 2
                    pe.wait_ge(th_ready, s + 1)
                    if late(s, 2):
                        pe.wait_ge(thT_ready, s - 1)
                    for k in range(DC):
                        ins = pe.transpose(bank[4 + par][:, k * P:(k + 1) * P], th[:, par, k * P:(k + 1) * P], ident[:])
                    ins.then_inc(th_psum, 1)
                    if late(s, 2):
                        pe.wait_ge(y_ready, s - 1)
                    pe.wait_ge(w_in[slot], 16 * (EP + 1) * (r + 1))
                    pe.matmul(bank[6 + par], esel[:], bias[:, slot, :], start=True, stop=False, skip_group_check=True)
                    pe.wait_ge(thT_ready, s + 1)
                    for j in range(EP):
                        for k in range(DC):
                            ins = pe.matmul(bank[6 + par][j * PS:(j + 1) * PS, :], thT[:, par, k * P + j * PS:k * P + (j + 1) * PS],
                                            w[:, slot, j, k, :], start=False, stop=(k == DC - 1), skip_group_check=True)
                    ins.then_inc(y_psum, 1)
                staged(pe, ST, (0, run), unroll=RING)

            @block.scalar
            def _(act):
                def copy(s, par, r, again):
                    if again:
                        act.wait_ge(slot_psum, s - 1)
                    act.activation(xT[:, par], slots_in[:, :, bass.ds(s * P, P)], ACT.Copy).then_inc(copied, 1)
                pairs(act, ST, copy)

                def take(t, par, r, again):
                    hold(act, cs_psum, t + 1)
                    for n in range(2):
                        act.activation(shiftC[:, bass.ds((2 * t + n) * P, P)],
                                       psum[:, 2 + par, :].bitcast(BF16)[n * 2 * PS:(n + 1) * 2 * PS, 0:P],
                                       ACT.Copy).then_inc(cs_taken, 1)
                pairs(act, T // 2, take)
                rstd_root(act, roots, 5, smv[:, :, 1], rroot[:])

                def tanh(s, par, r, again):
                    act.wait_ge(a_ready, s + 1)
                    if again:
                        act.wait_ge(th_psum, s - 1)
                    act.activation(th[:, par, :], a[:, par, :], ACT.Tanh).then_inc(th_ready, 1)

                def turned(s, par, r, again):
                    act.wait_ge(th_psum, s + 1)
                    if again:
                        act.wait_ge(y_psum, s - 1)
                    act.activation(thT[:, par, :], bank[4 + par], ACT.Copy).then_inc(thT_ready, 1)

                def take_y(s, par, r, again):
                    act.wait_ge(y_psum, s + 1)
                    if again:
                        act.wait_ge(yl_ready, s - 1)
                    act.activation(y[:, par, :], bank[6 + par], ACT.Copy).then_inc(y_ready, 1)
                staged(act, ST, (0, tanh), (0, turned), (1, take_y))

            @block.vector
            def _(dve):
                own = Steps(dve, own_steps)
                dve.tensor_copy(identb[:], ident[:]).then_inc(setup, 1)
                own.then(dve.tensor_reduce(cm[:], cmax[:].rearrange("p t q s -> p t s q"), AX.X, ALU.max))
                own.then(dve.tensor_scalar(cs[:, :, 0:PS], cm[:], -1.0, None, ALU.mult))
                dve.scalar_tensor_tensor(out=cs[:, :, PS:], in0=cm[:], scalar=-1.0, in1=cs[:, :, 0:PS],
                                         op0=ALU.mult, op1=ALU.subtract).then_inc(cs_ready, 1)

                def clip(s, par, r, again):
                    dve.wait_ge(slot_psum, s + 1)
                    dve.tensor_scalar(slots[:, s, :], bank[par], -33000.0, 65000.0, ALU.max, ALU.min).then_inc(clipped, 1)
                    hold(dve, clipped, s + 1)
                    dve.bn_stats(sstats[:, s, :], slots[:, s, :])
                pairs(dve, ST, clip)
                own.then(dve.memset(a[:], 0.0))
                moments(own, dve, sstats, smv, rtmp[:])
                rstd_of(own, dve, roots, 5, smv[:, :, 1], rroot[:], rstd[:], rtmp[:])

                def normalise(s, par, r, again):
                    if again:
                        dve.wait_ge(th_ready, s - 1)
                    dve.tensor_scalar(a[:, par, :], slots[:, s, :], smv[:, s, 0:1], rstd[:, bass.ds(s, 1)],
                                      ALU.subtract, ALU.mult).then_inc(a_ready, 1)

                def parts(s, par, r, again):
                    dve.wait_ge(y_ready, s + 1)
                    dve.tensor_copy(yh[:, s, :], y[:, par, :]).then_inc(yh_ready, 1)
                    dve.wait_ge(yh_ready, s + 1)
                    dve.tensor_tensor(yl[:, s, :], y[:, par, :], yh[:, s, :], ALU.subtract).then_inc(yl_ready, 1)
                staged(dve, ST, (0, normalise), (2, parts))


def kernel(**inputs):
    import numpy as np
    import concourse.bacc as bacc
    from concourse.bass_utils import run_bass_kernel_spmd

    f32 = np.float32
    g = {k: np.asarray(v) for k, v in inputs.items()}
    lane = np.arange(P) % LANES
    ends = np.zeros((P, BW + 1), f32)
    ends[lane == 0, S - (BLK - 1) * BW] = 1.0
    arrays = {
        "x": g["x"], "ctx": g["ctx_1024"], "ctxT": g["ctx_1024"].transpose(0, 2, 1),
        "w_gateT": g["L0_ffn_w_gate"].T, "w_upT": g["L0_ffn_w_up"].T, "w_downT": g["L0_ffn_w_down"].T,
        "wq1": g["L1_xattn_Wq1"], "wk1": g["L1_xattn_Wk1"], "wv1": g["L1_xattn_Wv1"],
        "wk2": g["L1_xattn_Wk2"], "wv2": g["L1_xattn_Wv2"], "wo": g["L1_xattn_Wo"], "bo": np.broadcast_to(g["L1_xattn_bo"], (P, D)),
        "phiT": g["L1_ffn_phi_w"].T, "phi_b": g["L1_ffn_phi_b"][None],
        "expert_w": g["L1_ffn_expert_w"], "expert_b": g["L1_ffn_expert_b"],
        "ident_c": np.eye(P, dtype=f32),
        "lane_start_c": np.where(lane == BLK - 1, 0.0, BIG).astype(f32)[:, None],
        "path_end_c": ends,
        "head_sel_c": np.kron(np.tile(np.eye(HEADS, dtype=f32), (2, 1)), np.ones((1, P), f32)),
    }
    shaped = {
        "selD": np.kron(np.tile(np.eye(NE // 4, dtype=f32), (2, 1)), np.ones((1, PS), f32)),
        "selC": np.tile(np.eye(PS, dtype=f32), (2, P // PS)),
        "sel_sum": np.tile(np.eye(PS, dtype=f32), (P // PS, P // PS)),
        "esel": np.kron(np.eye(P // PS, dtype=f32), np.ones((1, PS), f32)),
        "phi_b_col": g["L1_ffn_phi_b"].reshape(SLOTS // P, P).T,
    }
    arrays.update(shaped)
    arrays = {f"in_{k}": np.ascontiguousarray(v) for k, v in arrays.items()}
    nc = bacc.Bacc("TRN2", target_bir_lowering=False, num_devices=1)
    args = [nc.dram_tensor(k, v.shape, mybir.dt.from_np(v.dtype), kind="ExternalInput").ap() for k, v in arrays.items()]
    consts = dict(zip(shaped, args[-len(shaped):]))
    args = args[:-len(shaped)]
    out = nc.dram_tensor("out", (B, S, D), F32, kind="ExternalOutput").ap()
    program(nc, *args, consts, out, 0)
    r = run_bass_kernel_spmd(nc, [arrays], core_ids=[0])
    return r.results[0]["out"]
```

```python
from contextlib import ExitStack

import concourse.bass as bass
from concourse import mybir

ALU = mybir.AluOpType
ACT = mybir.ActivationFunctionType
F32 = mybir.dt.float32
F16 = mybir.dt.float16
BF16 = mybir.dt.bfloat16
AX = mybir.AxisListType

P = 128
B, S, D = 16, 256, 256
T = B * S // P
DC = D // P
I = 120
INNER = 1024
HEADS, DH = 8, 64
HD = HEADS * DH
KEYS = S + I
NE, PS = 64, 32
SLOTS = NE * PS
LN_EPS = 1e-5
BIG = 1e30
WS = 64.0
ROUND = 12582912.0

BLK = 7
BW = 37
LANES = 8
STEPS = I + BLK - 1
UNROLL = 6


class Steps:

    def __init__(self, eng, sem):
        self.eng, self.sem, self.n = eng, sem, 0

    def did(self, ins):
        ins.then_inc(self.sem, 1)
        self.n = self.n + 1

    def seen(self):
        self.eng.wait_ge(self.sem, self.n)

    def then(self, ins):
        self.did(ins)
        self.seen()

    def rounds(self, start, i, each):
        self.n = start + i * each


def hold(eng, sem, value):
    eng.wait_ge(sem, value)
    eng.wait_ge(sem, 1)


def moments(own, dve, stats, mv, tmp):
    even, odd, mean, var = stats[:, :, 1], stats[:, :, 4], mv[:, :, 0], mv[:, :, 1]
    own.did(dve.tensor_tensor(mean, even, odd, ALU.add))
    own.did(dve.tensor_tensor(tmp, even, odd, ALU.subtract))
    own.then(dve.tensor_tensor(var, stats[:, :, 2], stats[:, :, 5], ALU.add))
    own.did(dve.tensor_scalar(mean, mean, 0.5, None, ALU.mult))
    own.then(dve.tensor_tensor(tmp, tmp, tmp, ALU.mult))
    own.then(dve.tensor_scalar(tmp, tmp, 0.25, None, ALU.mult))
    own.then(dve.scalar_tensor_tensor(out=var, in0=var, scalar=1.0 / D, in1=tmp, op0=ALU.mult, op1=ALU.add))


def pairs(eng, n, body):
    body(0, 0, 0, False)
    body(1, 1, 0, False)
    with eng.Fori(1, n // 2) as i:
        body(2 * i, 0, i, True)
        body(2 * i + 1, 1, i, True)


def staged(eng, n, *stages, unroll=2):
    deepest = max(lag for lag, _ in stages)
    head = -(-(deepest + unroll) // unroll) * unroll

    def static(j):
        for lag, body in stages:
            b = j - lag
            if 0 <= b < n:
                body(b, b % unroll, b // unroll, b >= unroll)
    for j in range(head):
        static(j)
    with eng.Fori(head // unroll, n // unroll) as i:
        for at in range(unroll):
            for lag, body in stages:
                body(unroll * i + (at - lag), (at - lag) % unroll, i + (at - lag) // unroll, True)
    for j in range(n, n + deepest):
        static(j)


def late(b, least):
    return not isinstance(b, int) or b >= least


def block_width(k):
    return min(BW, S - k * BW)


def program(nc, x, ctx, ctxT, w_gateT, w_upT, w_downT, wq1, wk1, wv1, wk2, wv2, wo, bo, phiT, phi_b,
            expert_w, expert_b, ident_c, lane_start_c, path_end_c, head_sel_c, consts, out, stop):
    cost_d = nc.dram_tensor("cost_d", [B, I, S], F32, kind="Internal").ap()
    path_d = nc.dram_tensor("path_d", [B, I, S], F32, kind="Internal").ap()
    with ExitStack() as top:
        resid = top.enter_context(nc.sbuf_tensor("resid", [P, T, D], F32))
        ident = top.enter_context(nc.sbuf_tensor("ident", [P, P], F32))
        psum = top.enter_context(nc.psum_tensor("psum", [P, 8, 512], F32))
        ps = [psum[:, i, :] for i in range(8)]
        mv = top.enter_context(nc.sbuf_tensor("mv", [P, T, 2], F32))
        stats = top.enter_context(nc.sbuf_tensor("stats", [P, T, 6], F32))
        x_in = top.enter_context(nc.semaphore("x_in"))
        roots = [top.enter_context(nc.semaphore(name)) for name in ("var_ready", "std_ready")]
        with ExitStack() as for_attention:
            w_parts = [[for_attention.enter_context(nc.sbuf_tensor(f"w_{n}_{part}", [P, DC, HD], F16)) for part in "hl"]
                       for n in range(5)]
            with ExitStack() as for_ffn:
                w_f = [for_ffn.enter_context(nc.sbuf_tensor(f"w{n}_f", [P, DC * INNER], F32)) for n in range(3)]
                w_in = for_ffn.enter_context(nc.semaphore("ffn_w_in"))
                align(nc, ps, resid, mv, stats, ident, roots, x_in, x, ctx, ctxT, ident_c, lane_start_c, path_end_c,
                      cost_d, path_d, (w_gateT, w_upT, w_downT), w_f, w_in, (wq1, wk1, wv1, wk2, wv2), w_parts)
                if stop != 1:
                    ffn(nc, psum, resid, mv, stats, ident, roots, w_f, w_in)
            if stop not in (1, 2):
                attention(nc, psum, resid, mv, stats, ident, roots, ctxT, w_parts, wo, bo, head_sel_c)
        if stop == 0:
            moe(nc, psum, resid, mv, stats, ident, roots, phiT, phi_b, expert_w, expert_b, consts, out)
            return
        done = top.enter_context(nc.semaphore("out_written"))
        with nc.Block() as block:
            @block.sync
            def _(sp):
                sp.dma_start(out.rearrange("b (h p) d -> p (b h) d", p=P), resid[:]).then_inc(done, 16)
                sp.wait_ge(done, 16)


def shift_lanes(dve, out, src, by):
    inside = [LANES - 1 if n == LANES - 1 else (n + by) % LANES for n in range(LANES)]
    return dve.stream_shuffle(out, src, [base + n for base in range(0, 32, LANES) for n in inside])


def rstd_root(act, roots, nth, var, root):
    var_ready, root_ready = roots
    act.wait_ge(var_ready, nth)
    act.activation(root, var, ACT.Sqrt).then_inc(root_ready, 1)


def rstd_of(own, dve, roots, nth, var, root, rstd, tmp):
    var_ready, root_ready = roots
    dve.tensor_scalar(var, var, LN_EPS, None, ALU.add).then_inc(var_ready, 1)
    dve.wait_ge(var_ready, nth)
    dve.wait_ge(root_ready, nth)
    own.then(dve.reciprocal(rstd, root))
    own.then(dve.tensor_tensor(tmp, rstd, rstd, ALU.mult))
    own.then(dve.tensor_tensor(tmp, tmp, var, ALU.mult))
    own.then(dve.tensor_scalar(tmp, tmp, -0.5, 1.5, ALU.mult, ALU.add))
    own.then(dve.tensor_tensor(rstd, rstd, tmp, ALU.mult))


def align(nc, ps, resid, mv, stats, ident, roots, x_in, x, ctx, ctxT, ident_c, lane_start_c, path_end_c, cost_d, path_d,
          ffn_w, w_f, w_in, attention_w, w_parts):
    with ExitStack() as c:
        def sb(name, shape, dt=F32):
            return c.enter_context(nc.sbuf_tensor(name, shape, dt))

        def sem(name):
            return c.enter_context(nc.semaphore(name))

        ones = sb("ones", [P, I])
        rstd = sb("rstd", [P, T])
        rtmp = sb("rtmp", [P, T])
        rroot = sb("rroot", [P, T])
        xn = sb("xn", [P, 2, 2, D])
        xnT = sb("xnT", [P, 2, DC, S])
        xsq = sb("xsq", [P, 2, DC, S])
        ctx_all = sb("ctx_all", [I, B, D])
        ctxTb = sb("ctxTb", [P, 2, DC, I])
        w_stage = sb("w_stage", [P, DC, HD])
        csq = sb("csq", [I, D])
        scr = sb("scr", [P, 3, S])
        aa = sb("aa", [I, B])
        d2 = sb("d2", [P, 2, S])
        root = sb("root", [P, 2, S])
        dist = sb("dist", [P, 2, S])
        cost = sb("cost", [P, STEPS, BW])
        acc = sb("acc", [P, STEPS + 1, BW + 1])
        row = sb("row", [P, 2, BW + 1])
        least = sb("least", [P, BW])
        pick = sb("pick", [P, STEPS, 2, BW], BF16)
        left = sb("left", [P, STEPS, BW + 1], BF16)
        tie = sb("tie", [P, STEPS, BW], BF16)
        marks = sb("marks", [P, 2, BW + 1])
        flow = sb("flow", [P, 2, BW + 2])
        inflow = sb("inflow", [P, BW + 1])
        edge = sb("edge", [P, 1])
        path = cost
        masks = acc[0:I].rearrange("p s w -> p (s w)")[:, 0:B * S].rearrange("p (b s) -> p b s", s=S)

        QB = B // 4
        consts_in, start_in, ctx_in = sem("consts_in"), sem("start_in"), sem("ctx_in")
        ctxT_in = [sem(f"ctxT_in{n}") for n in range(2)]
        ones_set, cost_set = sem("ones_set"), sem("cost_set")
        xn_ready, xnT_psum, xnT_ready = sem("xn_ready"), sem("xnT_psum"), sem("xnT_ready")
        dots_psum, aa_ready, d2_ready, root_ready, dist_ready = (
            sem("dots_psum"), sem("aa_ready"), sem("d2_ready"), sem("root_ready"), sem("dist_ready"))
        cost_out, cost_in = [sem(f"cost_out{n}") for n in range(2)], sem("cost_in")
        row_ready, row_saved, mark_ready, mark_saved = (
            sem("row_ready"), sem("row_saved"), sem("mark_ready"), sem("mark_saved"))
        path_out, mask_in, gathered, resid_ready = (
            sem("path_out"), [sem(f"mask_in{n}") for n in range(4)], sem("gathered"), sem("resid_ready"))
        stage_in, stage_steps = sem("stage_in"), sem("stage_steps")
        dve_steps, sum_steps, newton_steps = sem("dve_steps"), sem("sum_steps"), sem("newton_steps")

        xt_ps = [ps[0], ps[1]]
        dot_ps = [ps[2], ps[3]]

        def skewed_costs(eng, half):
            eng.wait_ge(cost_set, 1)
            for par in range(2):
                eng.wait_ge(cost_out[par], 16 * B // 2)
            for k in range(half, BLK, 2):
                w = block_width(k)
                eng.dma_start(cost[BLK - 1 - k:P:LANES, k:k + I, 0:w],
                              cost_d[:, :, k * BW:k * BW + w]).then_inc(cost_in, 16)

        def store_paths(eng, half):
            eng.wait_ge(mark_saved, STEPS)
            for k in range(half, BLK, 2):
                w = block_width(k)
                eng.dma_start(path_d[:, :, k * BW:k * BW + w],
                              path[BLK - 1 - k:P:LANES, k:k + I, 0:w]).then_inc(path_out, 16)

        with nc.Block() as block:
            @block.sync
            def _(sp):
                for q in range(4):
                    sp.dma_start(resid[:, 8 * q:8 * q + 8, :],
                                 x.rearrange("b (h p) d -> p (b h) d", p=P)[:, 8 * q:8 * q + 8, :]).then_inc(x_in, 16)
                sp.dma_start(ident[:], ident_c).then_inc(consts_in, 16)
                sp.dma_start(row[:, 0, 0:1], lane_start_c).then_inc(start_in, 16)
                sp.dma_start(inflow[:], path_end_c).then_inc(start_in, 16)
                sp.dma_start(ctx_all[:], ctx.rearrange("b i d -> i b d")).then_inc(ctx_in, 16)

                def load(b, par, r, again):
                    if again:
                        sp.wait_ge(dots_psum, b - 1)
                    sp.dma_start(ctxTb[:, par], ctxT[b].rearrange("(c p) i -> p c i", p=P)).then_inc(ctxT_in[par], 16)
                pairs(sp, B, load)
                skewed_costs(sp, 0)
                for f, src in zip(w_f, ffn_w):
                    rows = src.shape[0] // P
                    sp.dma_start(f[:].rearrange("p (c n) -> p c n", c=rows), src.rearrange("(c p) n -> p c n", p=P)).then_inc(w_in, 16)
                store_paths(sp, 0)
                sp.wait_ge(path_out, 16 * BLK)
                for n in range(4):
                    sp.dma_start(masks[:, QB * n:QB * (n + 1), :],
                                 path_d[QB * n:QB * (n + 1)].rearrange("b i s -> i b s")).then_inc(mask_in[n], 16)

            @block.gpsimd
            def _(pool):
                pool.memset(cost[:], BIG).then_inc(cost_set, 1)

                def store(b, par, r, again):
                    pool.wait_ge(dist_ready, b + 1)
                    pool.dma_start(cost_d[b], dist[0:I, par, :]).then_inc(cost_out[par], 16)
                pairs(pool, B, store)

                own = Steps(pool, stage_steps)
                for n, (src, (high, low)) in enumerate(zip(attention_w, w_parts)):
                    if n:
                        own.seen()
                    pool.dma_start(w_stage[:], src.rearrange("(c p) n -> p c n", p=P)).then_inc(stage_in, 16)
                    pool.wait_ge(stage_in, 16 * (n + 1))
                    own.then(pool.tensor_scalar(w_stage[:], w_stage[:], WS, None, ALU.mult))
                    own.then(pool.tensor_copy(high[:], w_stage[:]))
                    own.did(pool.tensor_tensor(low[:], w_stage[:], high[:], ALU.subtract))
            @block.tensor
            def _(pe):
                pe.wait_ge(consts_in, 16)
                pe.wait_ge(ones_set, 1)

                def turn(b, par, r, again):
                    pe.wait_ge(xn_ready, 2 * b + 2)
                    for h in range(2):
                        for k in range(DC):
                            ins = pe.transpose(xt_ps[par][:, k * S + h * P:k * S + (h + 1) * P],
                                               xn[:, par, h, k * P:(k + 1) * P], ident[:])
                    ins.then_inc(xnT_psum, 1)

                def products(b, par, r, again):
                    pe.wait_ge(ctxT_in[par], (r + 1) * 16)
                    pe.wait_ge(xnT_ready, (b + 1) * 2)
                    if again:
                        pe.wait_ge(d2_ready, b - 1)
                    for k in range(DC):
                        pe.matmul(dot_ps[par][0:I, 0:S], ctxTb[:, par, k, :], xnT[:, par, k, :],
                                  start=(k == 0), stop=(k == DC - 1))
                    for k in range(DC):
                        ins = pe.matmul(dot_ps[par][0:I, S:2 * S], ones[:], xsq[:, par, k, :],
                                        start=(k == 0), stop=(k == DC - 1))
                    ins.then_inc(dots_psum, 1)
                staged(pe, B, (0, turn), (1, products))

                for b in range(B):
                    if b % QB == 0:
                        pe.wait_ge(mask_in[b // QB], 16)
                    if b >= 2:
                        pe.wait_ge(resid_ready, b - 1)
                    for h in range(2):
                        ins = pe.matmul(xt_ps[b % 2][:, h * D:(h + 1) * D], masks[:, b, h * P:(h + 1) * P],
                                        ctx_all[:, b, :], start=True, stop=True)
                    ins.then_inc(gathered, 1)

            @block.scalar
            def _(act):
                rstd_root(act, roots, 1, mv[:, :, 1], rroot[:])

                def transposed(b, par, r, again):
                    act.wait_ge(xnT_psum, b + 1)
                    act.activation(xnT[:, par].rearrange("p c s -> p (c s)"), xt_ps[par], ACT.Copy).then_inc(xnT_ready, 1)
                    act.activation(xsq[:, par].rearrange("p c s -> p (c s)"), xt_ps[par], ACT.Square).then_inc(xnT_ready, 1)

                def square_root(b, par, r, again):
                    if again:
                        act.wait_ge(dist_ready, b - 1)
                    act.wait_ge(d2_ready, b + 1)
                    act.activation(root[0:I, par, :], d2[0:I, par, :], ACT.Sqrt).then_inc(root_ready, 1)
                staged(act, B, (0, transposed), (1, square_root))
                skewed_costs(act, 1)

                act.wait_ge(row_ready, 1)
                act.activation(acc[:, 0, :], row[:, 0, :], ACT.Copy).then_inc(row_saved, 1)
                with act.Fori(0, STEPS // UNROLL) as i:
                    for n in range(UNROLL):
                        act.wait_ge(row_ready, UNROLL * i + n + 2)
                        act.activation(acc[:, UNROLL * i + n + 1, :], row[:, 1 - n % 2, :], ACT.Copy).then_inc(row_saved, 1)

                with act.Fori(0, STEPS // UNROLL) as i:
                    for n in range(UNROLL):
                        act.wait_ge(mark_ready, UNROLL * i + n + 1)
                        act.activation(path[:, STEPS - 1 - n - UNROLL * i, :], marks[:, n % 2, 1:], ACT.Copy).then_inc(mark_saved, 1)
                store_paths(act, 1)

            @block.vector
            def _(dve):
                own = Steps(dve, dve_steps)
                dve.memset(ones[:], 1.0).then_inc(ones_set, 1)
                dve.wait_ge(x_in, 64)
                for t in range(T):
                    own.did(dve.bn_stats(stats[:, t, :], resid[:, t, :]))
                own.seen()
                moments(own, dve, stats, mv, rtmp[:])
                rstd_of(own, dve, roots, 1, mv[:, :, 1], rroot[:], rstd[:], rtmp[:])
                start = own.n

                def normalise(b, par, r, again):
                    if again:
                        dve.wait_ge(xnT_psum, b - 1)
                    for h in range(2):
                        t = 2 * b + h
                        dve.tensor_scalar(xn[:, par, h, :], resid[:, t, :], mv[:, t, 0:1], rstd[:, bass.ds(t, 1)],
                                          ALU.subtract, ALU.mult).then_inc(xn_ready, 1)

                sums, newton = Steps(dve, sum_steps), Steps(dve, newton_steps)
                dve.wait_ge(ctx_in, 16)
                for b in range(B):
                    if b:
                        dve.wait_ge(aa_ready, b)
                    dve.tensor_tensor_reduce(csq[:], ctx_all[:, b, :], ctx_all[:, b, :], 1.0, 0.0,
                                             ALU.mult, ALU.add, aa[:, b:b + 1]).then_inc(aa_ready, 1)
                dve.wait_ge(aa_ready, B)

                def squares(b, par, rnd, again):
                    sums.rounds(0, b, 2)
                    if late(b, 1):
                        dve.wait_ge(d2_ready, b)
                    dve.wait_ge(dots_psum, b + 1)
                    s = scr[0:I, 0, :]
                    sums.then(dve.tensor_scalar(s, dot_ps[par][0:I, S:2 * S], aa[:, bass.ds(b, 1)], None, ALU.add))
                    sums.then(dve.scalar_tensor_tensor(out=s, in0=dot_ps[par][0:I, 0:S], scalar=-2.0, in1=s,
                                                       op0=ALU.mult, op1=ALU.add))
                    dve.tensor_scalar(d2[0:I, par, :], s, 0.0, None, ALU.max).then_inc(d2_ready, 1)

                def distances(b, par, rnd, again):
                    newton.rounds(0, b, 5)
                    d, r, s, y = (d2[0:I, par, :], root[0:I, par, :], scr[0:I, 1, :], scr[0:I, 2, :])
                    dve.wait_ge(d2_ready, b + 1)
                    dve.wait_ge(root_ready, b + 1)
                    if late(b, 1):
                        dve.wait_ge(dist_ready, b)
                    newton.did(dve.tensor_tensor(s, r, r, ALU.mult))
                    newton.then(dve.tensor_scalar(y, r, 1e-18, 2.0, ALU.max, ALU.mult))
                    newton.did(dve.tensor_tensor(s, d, s, ALU.subtract))
                    newton.then(dve.reciprocal(y, y))
                    newton.then(dve.tensor_tensor(s, s, y, ALU.mult))
                    if again:
                        dve.wait_ge(cost_out[par], 16 * rnd)
                    dve.tensor_tensor(dist[0:I, par, :], r, s, ALU.add).then_inc(dist_ready, 1)
                staged(dve, B, (0, normalise), (2, squares), (3, distances))
                own.n = start

                own.did(dve.memset(row[:, 0, 1:], BIG))
                own.did(dve.memset(row[:, 1, :], BIG))
                dve.wait_ge(start_in, 32)
                own.seen()
                dve.sem_inc(row_ready, 1)
                dve.wait_ge(cost_in, 16 * BLK)
                start = own.n

                def forth(s, par, first=False):
                    own.rounds(start, s, 2)
                    old, new = row[:, par], row[:, 1 - par]
                    if not first:
                        dve.wait_ge(row_saved, s)
                    dve.wait_ge(row_ready, s + 1)
                    own.did(dve.tensor_tensor(least[:], old[:, 1:], old[:, 0:BW], ALU.min))
                    own.then(shift_lanes(dve, new[:, 0:1], old[:, BW:BW + 1], 1))
                    dve.tensor_tensor_scan(new[:, 1:], least[:], cost[:, s, :], new[:, 0:1],
                                           ALU.min, ALU.add).then_inc(row_ready, 1)
                for s in range(UNROLL):
                    forth(s, s % 2, s == 0)
                with dve.Fori(1, STEPS // UNROLL) as i:
                    for s in range(UNROLL):
                        forth(UNROLL * i + s, s % 2)
                own.rounds(start, STEPS, 2)

                above, diag, lft = acc[:, 0:STEPS, 1:], acc[:, 0:STEPS, 0:BW], acc[:, 1:, 0:BW]
                up_, dg_, lf_ = pick[:, :, 0, :], pick[:, :, 1, :], left[:, :, BW:0:-1]
                dve.wait_ge(row_saved, STEPS + 1)
                own.did(dve.memset(left[:, :, 0:1], 1.0))
                own.then(dve.tensor_tensor(cost[:], above, lft, ALU.min))
                own.did(dve.tensor_tensor(dg_, diag, cost[:], ALU.is_le))
                own.then(dve.tensor_tensor(tie[:], above, lft, ALU.is_le))
                own.then(dve.tensor_tensor(up_, tie[:], dg_, ALU.is_gt))
                own.then(dve.tensor_tensor(lf_, up_, dg_, ALU.is_equal))

                own.did(dve.memset(flow[:], 0.0))
                own.did(dve.memset(marks[:], 0.0))
                own.did(dve.memset(edge[:], 0.0))
                own.seen()
                dve.tensor_tensor_scan(marks[:, 0, ::-1], left[:, STEPS - 1, :], inflow[:, ::-1], edge[:],
                                       ALU.mult, ALU.add).then_inc(mark_ready, 1)
                dve.wait_ge(mark_ready, 1)
                start = own.n

                def back(n, par, s):
                    own.rounds(start, n - 1, 3)
                    old, new = marks[:, 1 - par], marks[:, par]
                    own.did(dve.tensor_tensor(flow[:, :, 1:BW + 1], old[:, 1:].unsqueeze(1).to_broadcast([P, 2, BW]),
                                              pick[:, s + 1, :, :], ALU.mult))
                    own.then(shift_lanes(dve, edge[:], old[:, 0:1], -1))
                    own.then(dve.tensor_tensor(inflow[:], flow[:, 0, 0:BW + 1], flow[:, 1, 1:BW + 2], ALU.add))
                    dve.wait_ge(mark_saved, n)
                    dve.tensor_tensor_scan(new[:, ::-1], left[:, s, :], inflow[:, ::-1], edge[:],
                                           ALU.mult, ALU.add).then_inc(mark_ready, 1)
                    dve.wait_ge(mark_ready, n + 1)
                for n in range(1, UNROLL):
                    back(n, n % 2, STEPS - 1 - n)
                with dve.Fori(1, STEPS // UNROLL) as i:
                    s = dve.snap(STEPS - 1 - UNROLL * i)
                    for n in range(UNROLL):
                        back(UNROLL * i + n, n % 2, s - n)

                def add(b, par, r, again):
                    dve.wait_ge(gathered, b + 1)
                    both = resid[:, bass.ds(2 * b, 2), :].rearrange("p h d -> p (h d)")
                    dve.tensor_tensor(both, both, xt_ps[par], ALU.add).then_inc(resid_ready, 1)
                    hold(dve, resid_ready, b + 1)
                    for h in range(2):
                        dve.bn_stats(stats[:, 2 * b + h, :], resid[:, 2 * b + h, :])
                pairs(dve, B, add)


def ffn(nc, psum, resid, mv, stats, ident, roots, w_f, w_in):
    KC = INNER // P
    with ExitStack() as c:
        def sb(name, shape, dt=F32):
            return c.enter_context(nc.sbuf_tensor(name, shape, dt))

        def sem(name):
            return c.enter_context(nc.semaphore(name))

        w_t = [sb(f"w{n}_t", [P, DC * INNER]) for n in range(3)]
        w_q = [sb(f"w{n}_q", [P, DC * INNER], BF16) for n in range(3)]
        ones = sb("f_ones", [P, P])
        identb = sb("f_identb", [P, P], BF16)
        wabs = sb("wabs", [P, 3])
        wmean = sb("wmean", [P, 3])
        wscale = sb("wscale", [P, 3])
        rstd, rtmp, rroot = sb("f_rstd", [P, T]), sb("f_rtmp", [P, T]), sb("f_rroot", [P, T])
        xn = sb("f_xn", [P, 2, D])
        xr = sb("f_xr", [P, 2, D])
        xq = sb("f_xq", [P, 2, D], BF16)
        xqT = sb("f_xqT", [P, 2, D], BF16)
        amax = sb("f_amax", [P, 2, 1])
        aq = sb("f_aq", [P, 2, 1])
        ad = sb("f_ad", [P, 2, 2])
        silu = sb("f_silu", [P, 2, INNER])
        h = sb("f_h", [P, 2, INNER])
        hr = sb("f_hr", [P, 2, INNER])
        hq = sb("f_hq", [P, 2, INNER], BF16)
        hqT = sb("f_hqT", [P, 2, INNER], BF16)
        magic = sb("f_magic", [P, 1])
        hmax = sb("f_hmax", [P, 2, 1])
        hs = sb("f_hs", [P, 2, 1])
        hd = sb("f_hd", [P, 4, 1])

        setup, w_sums, w_ready = sem("f_setup"), sem("w_sums"), sem("w_ready")
        xq_ready, xq_psum, xqT_ready = sem("xq_ready"), sem("xq_psum"), sem("xqT_ready")
        wide_psum, silu_ready, h_ready = sem("wide_psum"), sem("silu_ready"), sem("h_ready")
        hr_ready, hq_ready, hq_psum, hqT_ready = sem("hr_ready"), sem("hq_ready"), sem("hq_psum"), sem("hqT_ready")
        hs_ready, h_rounded = sem("hs_ready"), sem("h_rounded")
        down_psum, resid_new = sem("down_psum"), sem("resid_new")
        a_steps, b_steps = sem("f_a_steps"), sem("f_b_steps")

        gate_ps = psum[:, 0:2, :].rearrange("p a n -> p (a n)")
        up_ps = psum[:, 2:4, :].rearrange("p a n -> p (a n)")
        xq_ps = psum[:, 4, :].bitcast(BF16)
        hq_ps = psum[:, 5, :].bitcast(BF16)
        down_ps = [psum[:, 6, 0:D], psum[:, 7, 0:D]]

        with nc.Block() as block:
            @block.gpsimd
            def _(pool):
                def settle(b, par, r, again):
                    pool.wait_ge(hr_ready, b + 1)
                    pool.tensor_tensor(hr[:, par, :], hr[:, par, :], magic[:].to_broadcast([P, INNER]),
                                       ALU.add).then_inc(h_rounded, 1)
                    if again:
                        pool.wait_ge(hq_psum, b - 1)
                    pool.wait_ge(h_rounded, b + 2)
                    pool.tensor_tensor(hq[:, par, :], hr[:, par, :], magic[:].to_broadcast([P, INNER]),
                                       ALU.subtract).then_inc(hq_ready, 1)
                pool.memset(magic[:], ROUND).then_inc(h_rounded, 1)
                pool.wait_ge(h_rounded, 1)
                pairs(pool, T, settle)

            @block.tensor
            def _(pe):
                pe.wait_ge(setup, 5)
                pe.matmul(psum[:, 7, 0:3], ones[:], wabs[:], start=True, stop=True).then_inc(w_sums, 1)
                pe.wait_ge(w_ready, 3)

                def turn_x(b, par, r, again):
                    pe.wait_ge(xq_ready, b + 1)
                    for k in range(DC):
                        ins = pe.transpose(xq_ps[:, k * P:(k + 1) * P], xq[:, par, k * P:(k + 1) * P], identb[:])
                    ins.then_inc(xq_psum, 1)

                def widen(b, par, r, again):
                    pe.wait_ge(xqT_ready, b + 1)
                    if again:
                        pe.wait_ge(h_ready, b)
                    elif par:
                        pe.wait_ge(h_ready, 1)
                    for k in range(DC):
                        for m, bank in ((0, gate_ps), (1, up_ps)):
                            for n in range(INNER // 512):
                                ins = pe.matmul(bank[:, n * 512:(n + 1) * 512], xqT[:, par, k * P:(k + 1) * P],
                                                w_q[m][:, k * INNER + n * 512:k * INNER + (n + 1) * 512],
                                                start=(k == 0), stop=(k == DC - 1))
                    ins.then_inc(wide_psum, 1)

                def turn_h(b, par, r, again):
                    pe.wait_ge(hq_ready, b + 1)
                    for k in range(KC):
                        ins = pe.transpose(hq_ps[:, k * P:(k + 1) * P], hq[:, par, k * P:(k + 1) * P], identb[:])
                    ins.then_inc(hq_psum, 1)

                def narrow(b, par, r, again):
                    pe.wait_ge(hqT_ready, b + 1)
                    if again:
                        pe.wait_ge(resid_new, b - 1)
                    for k in range(KC):
                        ins = pe.matmul(down_ps[par], hqT[:, par, k * P:(k + 1) * P], w_q[2][:, k * D:(k + 1) * D],
                                        start=(k == 0), stop=(k == KC - 1))
                    ins.then_inc(down_psum, 1)
                staged(pe, T, (0, turn_x), (3, turn_h), (0, widen), (3, narrow))

            @block.scalar
            def _(act):
                rstd_root(act, roots, 2, mv[:, :, 1], rroot[:])

                def turned_x(b, par, r, again):
                    act.wait_ge(xq_psum, b + 1)
                    act.activation(xqT[:, par, :], xq_ps[:, 0:D], ACT.Copy).then_inc(xqT_ready, 1)

                def gate(b, par, r, again):
                    act.wait_ge(wide_psum, b + 1)
                    act.activation(silu[:, par, :], gate_ps, ACT.Silu, scale=ad[:, par, 0:1]).then_inc(silu_ready, 1)

                def scale(b, par, r, again):
                    if again:
                        act.wait_ge(hq_ready, b - 1)
                    act.wait_ge(hs_ready, b + 1)
                    act.activation(hr[:, par, :], h[:, par, :], ACT.Copy, scale=hs[:, par, :]).then_inc(hr_ready, 1)

                def turned_h(b, par, r, again):
                    act.wait_ge(hq_psum, b + 1)
                    act.activation(hqT[:, par, :], hq_ps, ACT.Copy).then_inc(hqT_ready, 1)
                staged(act, T, (0, turned_x), (3, turned_h), (0, gate), (1, scale))

            @block.vector
            def _(dve):
                one, two = Steps(dve, a_steps), Steps(dve, b_steps)
                dve.memset(ones[:], 1.0).then_inc(setup, 1)
                dve.tensor_copy(identb[:], ident[:]).then_inc(setup, 1)
                dve.wait_ge(w_in, 48)
                for n in range(3):
                    dve.tensor_reduce(wabs[:, n:n + 1], w_f[n][:], AX.X, ALU.add, apply_absolute_value=True).then_inc(setup, 1)
                moments(one, dve, stats, mv, rtmp[:])
                rstd_of(one, dve, roots, 2, mv[:, :, 1], rroot[:], rstd[:], rtmp[:])
                dve.wait_ge(w_sums, 1)
                one.then(dve.tensor_scalar(wmean[:], psum[:, 7, 0:3], 1.0 / (D * INNER), 1e-5, ALU.mult, ALU.max))
                one.then(dve.reciprocal(wscale[:], wmean[:]))
                for n in range(3):
                    one.then(dve.tensor_scalar(w_t[n][:], w_f[n][:], wscale[:, n:n + 1], ROUND, ALU.mult, ALU.add))
                    one.then(dve.tensor_scalar(w_t[n][:], w_t[n][:], ROUND, -1.0, ALU.subtract, ALU.max))
                    dve.tensor_scalar(w_q[n][:], w_t[n][:], 1.0, None, ALU.min).then_inc(w_ready, 1)
                base = one.n

                def quantise(b, slot, r, again):
                    par = slot % 2
                    one.rounds(base, b, 6)
                    one.then(dve.tensor_scalar(xn[:, par, :], resid[:, b, :], mv[:, b, 0:1], rstd[:, bass.ds(b, 1)],
                                               ALU.subtract, ALU.mult))
                    one.then(dve.tensor_reduce(amax[:, par, :], xn[:, par, :], AX.X, ALU.max, apply_absolute_value=True))
                    one.then(dve.tensor_scalar(amax[:, par, :], amax[:, par, :], 1e-5, 1.0 / 127.0, ALU.max, ALU.mult))
                    one.did(dve.reciprocal(aq[:, par, :], amax[:, par, :]))
                    if late(b, 2):
                        dve.wait_ge(silu_ready, b - 1)
                    one.then(dve.tensor_scalar(ad[:, par, :], wmean[:, 0:2], amax[:, par, :], None, ALU.mult))
                    one.then(dve.tensor_scalar(xr[:, par, :], xn[:, par, :], aq[:, par, :], ROUND, ALU.mult, ALU.add))
                    if late(b, 2):
                        dve.wait_ge(xq_psum, b - 1)
                    dve.tensor_scalar(xq[:, par, :], xr[:, par, :], ROUND, 127.0, ALU.subtract, ALU.min).then_inc(xq_ready, 1)

                def product(b, slot, r, again):
                    par = slot % 2
                    two.rounds(0, b, 3)
                    if late(b, 2):
                        dve.wait_ge(hr_ready, b - 1)
                    dve.wait_ge(silu_ready, b + 1)
                    dve.scalar_tensor_tensor(out=h[:, par, :], in0=up_ps, scalar=ad[:, par, 1:2], in1=silu[:, par, :],
                                             op0=ALU.mult, op1=ALU.mult).then_inc(h_ready, 1)
                    dve.wait_ge(h_ready, b + 1)
                    two.then(dve.tensor_reduce(hmax[:, par, :], h[:, par, :], AX.X, ALU.max, apply_absolute_value=True))
                    two.then(dve.tensor_scalar(hmax[:, par, :], hmax[:, par, :], 1e-5, 1.0 / 127.0, ALU.max, ALU.mult))
                    dve.reciprocal(hs[:, par, :], hmax[:, par, :]).then_inc(hs_ready, 1)
                    two.did(dve.tensor_scalar(hd[:, slot, :], wmean[:, 2:3], hmax[:, par, :], None, ALU.mult))

                def add(b, slot, r, again):
                    par = slot % 2
                    dve.wait_ge(down_psum, b + 1)
                    dve.wait_ge(b_steps, 3 * (b + 1))
                    dve.scalar_tensor_tensor(out=resid[:, b, :], in0=down_ps[par], scalar=hd[:, slot, :], in1=resid[:, b, :],
                                             op0=ALU.mult, op1=ALU.add).then_inc(resid_new, 1)
                    hold(dve, resid_new, b + 1)
                    dve.bn_stats(stats[:, b, :], resid[:, b, :])
                staged(dve, T, (2, product), (0, quantise), (5, add), unroll=4)


def attention(nc, psum, resid, mv, stats, ident, roots, ctxT, w_parts, wo, bo, head_sel_c):
    VW = DH + 1
    PAIRS = HEADS // 2
    UNITS = 3 * PAIRS
    KT = DC + 1
    rows = [P, P, I]
    with ExitStack() as c:
        def sb(name, shape, dt=F32):
            return c.enter_context(nc.sbuf_tensor("t_" + name, shape, dt))

        def sem(name):
            return c.enter_context(nc.semaphore("t_" + name))

        wo_sb = sb("wo", [P, HD // P, D])
        bo_sb = sb("bo", [P, 2, D])
        sel_f = sb("sel_f", [2 * HEADS, HEADS * P])
        sel = sb("sel", [2 * HEADS, HEADS * P], BF16)
        identb = sb("identb", [P, P], BF16)
        rstd, rtmp, rroot = sb("rstd", [P, T]), sb("rtmp", [P, T]), sb("rroot", [P, T])
        xn = sb("xn", [P, 2, 2, D])
        xTh, xTl = sb("xTh", [P, DC, S], F16), sb("xTl", [P, DC, S], F16)
        ctxTb = sb("ctxTb", [P, 2, DC, I])
        cTh, cTl = sb("cTh", [P, 2, DC, I], F16), sb("cTl", [P, 2, DC, I], F16)
        qh, ql = [sb(n, [P, 2, HEADS // 2, S], F16) for n in ("qh", "ql")]
        kh, kl = [sb(n, [P, 2, HEADS // 2, KEYS], F16) for n in ("kh", "kl")]
        vh, vl = [sb(n, [P, 2, KT, HEADS, VW], F16) for n in ("vh", "vl")]
        top = sb("top", [P, 2, 2, HEADS])
        shift = sb("shift", [P, 2, 2, 2 * HEADS], BF16)
        shiftT = sb("shiftT", [2 * HEADS, 2, S], BF16)
        probs = sb("probs", [P, 2, 2 * KT, S])
        probs_h, probs_l = [sb(n, [P, 2, 2 * KT, S], F16) for n in ("probs_h", "probs_l")]
        rsum = sb("rsum", [P, 2, 4])
        o = sb("o", [P, 2, 2, HD])
        oT = sb("oT", [P, HD // P, S])

        w_in, setup = sem("w_in"), sem("setup")
        ctx_in = [sem(f"ctx_in{n}") for n in range(2)]
        cTh_ready, cTl_ready, biased = sem("cTh_ready"), sem("cTl_ready"), sem("biased")
        own_steps = sem("own_steps")
        xn_ready, xt_psum, xTh_ready, xTl_ready = sem("xn_ready"), sem("xt_psum"), sem("xTh_ready"), sem("xTl_ready")
        q_psum, k_psum, v_psum, qh_ready, kh_ready = sem("q_psum"), sem("k_psum"), sem("v_psum"), sem("qh_ready"), sem("kh_ready")
        bank_free = [sem(f"bank_free{n}") for n in range(2)]
        simA_psum, top_ready, high_ready, shift_ready = sem("simA_psum"), sem("top_ready"), sem("high_ready"), sem("shift_ready")
        probs_h_ready, probs_l_ready, vh_ready = sem("probs_h_ready"), sem("probs_l_ready"), sem("vh_ready")
        shift_psum, shiftT_ready = sem("shift_psum"), sem("shiftT_ready")
        unit_psum, half_psum, exp_ready, pv_psum, rsum_ready, o_ready = (
            sem("unit_psum"), sem("half_psum"), sem("exp_ready"), sem("pv_psum"), sem("rsum_ready"), sem("o_ready"))
        oT_psum, oT_ready, out_psum, added = sem("oT_psum"), sem("oT_ready"), sem("out_psum"), sem("added")

        unit_ps = [psum[:, n, :] for n in range(3)]
        SLOT = [[0, 1, 2], [4, 5, 3]]
        simA_ps = psum[:, 3:5, 0:KEYS]
        pv_ps = psum[:, 5, 0:4 * VW].rearrange("p (g n) -> p g n", n=VW)
        bank = [psum[:, 6, :], psum[:, 7, :]]
        shift_ps = psum[:, 3, :].bitcast(BF16)[0:2 * HEADS, 0:S]

        def unit(x, p, n):
            return x[0:I if n == 1 else P, p % 2, 2 * n:2 * n + 2, :].rearrange("p j s -> p (j s)")

        with nc.Block() as block:
            @block.sync
            def _(sp):
                sp.dma_start(wo_sb[:], wo.rearrange("(c p) n -> p c n", p=P)).then_inc(w_in, 16)
                for h in range(2):
                    sp.dma_start(bo_sb[:, h, :], bo).then_inc(w_in, 16)
                sp.dma_start(sel_f[:], head_sel_c).then_inc(w_in, 16)

                def load(b, par, r, again):
                    if again:
                        sp.wait_ge(cTl_ready, b - 1)
                    sp.dma_start(ctxTb[:, par], ctxT[b].rearrange("(c p) i -> p c i", p=P)).then_inc(ctx_in[par], 16)
                pairs(sp, B, load)

            @block.gpsimd
            def _(pool):
                def split_context(b, par, r, again):
                    if again:
                        pool.wait_ge(v_psum, KT * (b - 1))
                    pool.wait_ge(cTh_ready, b + 1)
                    pool.tensor_tensor(cTl[:, par], ctxTb[:, par], cTh[:, par], ALU.subtract).then_inc(cTl_ready, 1)
                    if not late(b, 1):
                        pool.wait_ge(w_in, 16 * 4)
                    pool.wait_ge(xn_ready, 2 * b + 2)
                    pool.tensor_tensor(resid[:, bass.ds(2 * b, 2), :], resid[:, bass.ds(2 * b, 2), :], bo_sb[:],
                                       ALU.add).then_inc(biased, 1)
                def low_probabilities(p):
                    def body(b, par, r, again):
                        for n in range(3):
                            pool.wait_ge(probs_h_ready, UNITS * b + 3 * p + n + 1)
                            whole, high, low = [unit(x, p, n) for x in (probs, probs_h, probs_l)]
                            pool.tensor_tensor(low, whole, high, ALU.subtract).then_inc(probs_l_ready, 1)
                    return body
                staged(pool, B, (0, split_context), *[(1, low_probabilities(p)) for p in range(PAIRS)])

            @block.tensor
            def _(pe):
                pe.wait_ge(setup, 3)

                def turn(b, par, r, again):
                    pe.wait_ge(xn_ready, 2 * b + 2)
                    if late(b, 1):
                        pe.wait_ge(bank_free[0], 5 * b)
                    if late(b, 3):
                        pe.wait_ge(added, b - 2)
                    for h in range(2):
                        for k in range(DC):
                            ins = pe.transpose(bank[0][:, k * S + h * P:k * S + (h + 1) * P],
                                               xn[:, par, h, k * P:(k + 1) * P], ident[:])
                    ins.then_inc(xt_psum, 1)

                def product(dst, lhs, rhs, last=True):
                    for k in range(DC):
                        for n, (a, c) in enumerate(((0, 0), (0, 1), (1, 0))):
                            ins = pe.matmul(dst, lhs(a, k), rhs(c, k), start=(k == 0 and n == 0), stop=(k == DC - 1 and n == 2))
                    return ins

                def project(b, par, r, again):
                    xT, cT = (xTh, xTl), (cTh, cTl)
                    pe.wait_ge(xTh_ready, b + 1)
                    pe.wait_ge(xTl_ready, b + 1)
                    if late(b, 1):
                        pe.wait_ge(bank_free[1], 5 * b)
                    for n in range(2):
                        if n == 1:
                            pe.wait_ge(bank_free[0], 5 * b + 1)
                        for m in range(2 * n, 2 * n + 2):
                            ins = product(bank[1 - n][:, (m % 2) * S:(m % 2 + 1) * S],
                                          lambda a, k: w_parts[0][a][:, k, m * P:(m + 1) * P], lambda c, k: xT[c][:, k, :])
                        ins.then_inc(q_psum, 1)
                    pe.wait_ge(cTl_ready, b + 1)
                    for m in range(HEADS // 2):
                        g = 1 - m % 2
                        pe.wait_ge(bank_free[g], 5 * b + 1 + (m + 1) // 2)
                        product(bank[g][:, 0:S], lambda a, k: w_parts[1][a][:, k, m * P:(m + 1) * P], lambda c, k: xT[c][:, k, :])
                        product(bank[g][:, S:KEYS], lambda a, k: w_parts[3][a][:, k, m * P:(m + 1) * P],
                                lambda c, k: cT[c][:, par, k, :]).then_inc(k_psum, 1)
                    for j in range(KT):
                        g = 1 - j % 2
                        pe.wait_ge(bank_free[g], 5 * b + 3 + (j + 1) // 2)
                        if j < DC:
                            ins = product(bank[g], lambda a, k: xT[a][:, k, j * P:(j + 1) * P], lambda c, k: w_parts[2][c][:, k, :])
                        else:
                            ins = product(bank[g][0:I, :], lambda a, k: cT[a][:, par, k, :], lambda c, k: w_parts[4][c][:, k, :])
                        ins.then_inc(v_psum, 1)

                def turn_output(b, par, r, again):
                    pe.wait_ge(o_ready, PAIRS * (b + 1))
                    for g in range(2):
                        pe.wait_ge(bank_free[g], 5 * (min(b + 3, B) if isinstance(b, int) else b + 3))
                    for m in range(HD // P):
                        for h in range(2):
                            ins = pe.transpose(bank[m // 2][:, (m % 2) * S + h * P:(m % 2) * S + (h + 1) * P],
                                               o[:, par, h, m * P:(m + 1) * P], ident[:])
                        if m % 2:
                            ins.then_inc(oT_psum, 1)

                def output(b, par, r, again):
                    pe.wait_ge(oT_ready, 2 * b + 2)
                    for h in range(2):
                        for k in range(HD // P):
                            ins = pe.matmul(bank[0][:, h * D:(h + 1) * D], oT[:, k, h * P:(h + 1) * P], wo_sb[:, k, :],
                                            start=(k == 0), stop=(k == HD // P - 1))
                    ins.then_inc(out_psum, 1)

                def scores_for_max(h):
                    lane, m = slice(64 * (h % 2), 64 * (h % 2) + 64), h // 2

                    def body(b, par, r, again):
                        if h == 0:
                            if late(b, 1):
                                pe.wait_ge(shiftT_ready, b)
                            pe.wait_ge(qh_ready, 2 * b + 2)
                            pe.wait_ge(kh_ready, 4 * b + 4)
                        if late(HEADS * b + h, 1):
                            pe.wait_ge(top_ready, HEADS * b + h)
                        for t in range(2):
                            ins = pe.matmul(simA_ps[:, t, :], qh[lane, par, m, t * P:(t + 1) * P], kh[lane, par, m, :],
                                            start=True, stop=True)
                        ins.then_inc(simA_psum, 1)
                    return body

                def score(b, par, h, j):
                    lane, m = slice(64 * (h % 2), 64 * (h % 2) + 64), h // 2
                    slot = SLOT[h % 2][j]
                    dst = unit_ps[slot // 2][0:rows[j], (slot % 2) * S:(slot % 2 + 1) * S]
                    keys = slice(j * P, j * P + rows[j])
                    pe.matmul(dst, sel[:, h * P:h * P + rows[j]], shiftT[:, par, :], start=True, stop=False)
                    pe.matmul(dst, kh[lane, par, m, keys], qh[lane, par, m, :], start=False, stop=False)
                    pe.matmul(dst, kh[lane, par, m, keys], ql[lane, par, m, :], start=False, stop=False)
                    return pe.matmul(dst, kl[lane, par, m, keys], qh[lane, par, m, :], start=False, stop=True)

                def unit_free(b, p, n):
                    if late(UNITS * b + 3 * p + n, 3):
                        pe.wait_ge(exp_ready, UNITS * b + 3 * p + n - 2)

                def scores_first(p):
                    def body(b, par, r, again):
                        if p == 0:
                            if not late(b, 1):
                                pe.wait_ge(setup, 4)
                            pe.wait_ge(bank_free[0], 5 * b + 5)
                            pe.wait_ge(bank_free[1], 5 * b + 5)
                            pe.wait_ge(shiftT_ready, b + 1)
                        unit_free(b, p, 0)
                        score(b, par, 2 * p, 0)
                        score(b, par, 2 * p, 1).then_inc(unit_psum, 1)
                        unit_free(b, p, 1)
                        score(b, par, 2 * p, DC).then_inc(half_psum, 1)
                    return body

                def scores_context(p):
                    def body(b, par, r, again):
                        pe.wait_ge(half_psum, PAIRS * b + p + 1)
                        score(b, par, 2 * p + 1, DC).then_inc(unit_psum, 1)
                    return body

                def scores_second(p):
                    def body(b, par, r, again):
                        unit_free(b, p, 2)
                        score(b, par, 2 * p + 1, 0)
                        score(b, par, 2 * p + 1, 1).then_inc(unit_psum, 1)
                    return body

                def values(p):
                    def body(b, par, r, again):
                        pe.wait_ge(probs_l_ready, UNITS * b + 3 * p + 3)
                        if late(PAIRS * b + p, 1):
                            pe.wait_ge(o_ready, PAIRS * b + p)
                        for h in (2 * p, 2 * p + 1):
                            for t in range(2):
                                for j in range(KT):
                                    for n, (a, c) in enumerate(((probs_h, vh), (probs_h, vl), (probs_l, vh))):
                                        ins = pe.matmul(pv_ps[:, 2 * (h % 2) + t, :],
                                                        a[0:rows[j], p % 2, SLOT[h % 2][j], t * P:(t + 1) * P],
                                                        c[0:rows[j], par, j, h, :], start=(j == 0 and n == 0),
                                                        stop=(j == KT - 1 and n == 2))
                        ins.then_inc(pv_psum, 1)
                    return body

                def shifts(b, par, r, again):
                    pe.wait_ge(shift_ready, b + 1)
                    for t in range(2):
                        ins = pe.transpose(shift_ps[:, t * P:(t + 1) * P], shift[:, par, t, :], identb[:])
                    ins.then_inc(shift_psum, 1)

                heads = []
                for p in range(PAIRS):
                    heads += [(0, scores_for_max(2 * p)), (1, scores_first(p))] + [(2, output)] * (p == 2)
                    heads += [(0, scores_for_max(2 * p + 1)), (1, scores_context(p)), (1, scores_second(p))]
                    heads += [(1, values(p - 1))] * (p > 0) + [(2, turn_output)] * (p == 1)
                staged(pe, B, (0, turn), (1, shifts), (2, values(PAIRS - 1)), (0, project), *heads)

            @block.scalar
            def _(act):
                rstd_root(act, roots, 3, mv[:, :, 1], rroot[:])

                act.wait_ge(w_in, 16 * 4)
                act.activation(sel[:], sel_f[:], ACT.Copy).then_inc(setup, 1)

                def turned(b, par, r, again):
                    if again:
                        act.wait_ge(v_psum, KT * (b - 1))
                    act.wait_ge(ctx_in[par], 16 * (r + 1))
                    act.activation(cTh[:, par], ctxTb[:, par], ACT.Copy).then_inc(cTh_ready, 1)
                    act.wait_ge(xt_psum, b + 1)
                    act.activation(xTh[:].rearrange("p c s -> p (c s)"), bank[0], ACT.Copy).then_inc(xTh_ready, 1)

                def projected(b, par, r, again):
                    for n in range(2):
                        act.wait_ge(q_psum, 2 * b + n + 1)
                        act.activation(qh[:, par, 2 * n:2 * n + 2, :].rearrange("p m s -> p (m s)"), bank[1 - n],
                                       ACT.Copy, scale=1.0 / WS).then_inc(qh_ready, 1)
                    for m in range(HEADS // 2):
                        act.wait_ge(k_psum, 4 * b + m + 1)
                        act.activation(kh[:, par, m, :], bank[1 - m % 2][:, 0:KEYS], ACT.Copy, scale=1.0 / WS).then_inc(kh_ready, 1)
                    if late(b, 2):
                        act.wait_ge(pv_psum, PAIRS * (b - 1))
                    for j in range(KT):
                        act.wait_ge(v_psum, KT * b + j + 1)
                        act.activation(vh[0:rows[j], par, j, :, 0:DH],
                                       bank[1 - j % 2][0:rows[j], :].rearrange("p (h d) -> p h d", d=DH),
                                       ACT.Copy, scale=1.0 / WS).then_inc(vh_ready, 1)

                def turned_output(b, par, r, again):
                    for n in range(2):
                        act.wait_ge(oT_psum, 2 * b + n + 1)
                        act.activation(oT[:, 2 * n:2 * n + 2, :].rearrange("p m s -> p (m s)"), bank[n], ACT.Copy).then_inc(oT_ready, 1)

                def exponentials(p):
                    def body(b, par, r, again):
                        for n in range(3):
                            act.wait_ge(unit_psum, UNITS * b + 3 * p + n + 1)
                            if late(PAIRS * b + p, 2):
                                act.wait_ge(probs_l_ready, UNITS * b + 3 * p + n - 5)
                            rows_n = I if n == 1 else P
                            act.activation(unit(probs, p, n), unit_ps[n][0:rows_n, :], ACT.Exp, scale=DH ** -0.5).then_inc(exp_ready, 1)
                            if n == 0 and late(PAIRS * b + p, 2):
                                act.wait_ge(pv_psum, PAIRS * b + p - 1)
                            act.wait_ge(exp_ready, UNITS * b + 3 * p + n + 1)
                            act.activation(unit(probs_h, p, n), unit(probs, p, n), ACT.Copy).then_inc(probs_h_ready, 1)
                    return body

                def shifted(b, par, r, again):
                    act.wait_ge(shift_psum, b + 1)
                    act.activation(shiftT[:, par, :], shift_ps, ACT.Copy).then_inc(shiftT_ready, 1)
                exps = [(1, exponentials(p)) for p in range(PAIRS)]
                staged(act, B, (0, turned), (1, shifted), (0, projected), *exps[:2], (2, turned_output), *exps[2:])

            @block.vector
            def _(dve):
                own = Steps(dve, own_steps)
                dve.memset(vh[:, :, :, :, DH:VW], 1.0).then_inc(setup, 1)
                dve.memset(vl[:, :, :, :, DH:VW], 0.0).then_inc(setup, 1)
                dve.tensor_copy(identb[:], ident[:]).then_inc(setup, 1)
                moments(own, dve, stats, mv, rtmp[:])
                rstd_of(own, dve, roots, 3, mv[:, :, 1], rroot[:], rstd[:], rtmp[:])

                def normalise(b, par, r, again):
                    if again:
                        dve.wait_ge(xt_psum, b - 1)
                    for h in range(2):
                        dve.tensor_scalar(xn[:, par, h, :], resid[:, 2 * b + h, :], mv[:, 2 * b + h, 0:1],
                                          rstd[:, bass.ds(2 * b + h, 1)], ALU.subtract, ALU.mult).then_inc(xn_ready, 1)

                def less(out, psum_of, high):
                    return dve.scalar_tensor_tensor(out=out, in0=psum_of, scalar=1.0 / WS, in1=high, op0=ALU.mult, op1=ALU.subtract)

                def low_x(b, par, r, again):
                    dve.wait_ge(xTh_ready, b + 1)
                    flat = [x[:].rearrange("p c s -> p (c s)") for x in (xTh, xTl)]
                    dve.tensor_tensor(flat[1], bank[0], flat[0], ALU.subtract).then_inc(xTl_ready, 1)
                    dve.wait_ge(xTl_ready, b + 1)
                    dve.sem_inc(bank_free[0], 1)

                def lows(b, par, r, again):
                    for n in range(2):
                        dve.wait_ge(qh_ready, 2 * b + n + 1)
                        flat = [x[:, par, 2 * n:2 * n + 2, :].rearrange("p m s -> p (m s)") for x in (qh, ql)]
                        less(flat[1], bank[1 - n], flat[0]).then_inc(bank_free[1 - n], 1)
                    for m in range(HEADS // 2):
                        dve.wait_ge(kh_ready, 4 * b + m + 1)
                        less(kl[:, par, m, :], bank[1 - m % 2][:, 0:KEYS], kh[:, par, m, :]).then_inc(bank_free[1 - m % 2], 1)
                    for j in range(KT):
                        dve.wait_ge(vh_ready, KT * b + j + 1)
                        less(vl[0:rows[j], par, j, :, 0:DH], bank[1 - j % 2][0:rows[j], :].rearrange("p (h d) -> p h d", d=DH),
                             vh[0:rows[j], par, j, :, 0:DH]).then_inc(bank_free[1 - j % 2], 1)

                def maxima(h):
                    def body(b, par, r, again):
                        dve.wait_ge(simA_psum, HEADS * b + h + 1)
                        dve.tensor_reduce(top[:, par, :, h], simA_ps, AX.X, ALU.max).then_inc(top_ready, 1)
                    return body

                def split(b, par, r, again):
                    dve.wait_ge(top_ready, HEADS * (b + 1))
                    if late(b, 2):
                        dve.wait_ge(shift_psum, b - 1)
                    dve.tensor_scalar(shift[:, par, :, 0:HEADS], top[:, par], -1.0, None, ALU.mult).then_inc(high_ready, 1)
                    dve.wait_ge(high_ready, b + 1)
                    dve.scalar_tensor_tensor(out=shift[:, par, :, HEADS:], in0=top[:, par], scalar=-1.0,
                                             in1=shift[:, par, :, 0:HEADS], op0=ALU.mult, op1=ALU.subtract).then_inc(shift_ready, 1)

                def normal(p):
                    def body(b, par, r, again):
                        dve.wait_ge(pv_psum, PAIRS * b + p + 1)
                        dve.reciprocal(rsum[:, p % 2, :], pv_ps[:, :, DH]).then_inc(rsum_ready, 1)
                        if p == 0 and late(b, 2):
                            dve.wait_ge(oT_psum, 2 * (b - 1))
                        dve.wait_ge(rsum_ready, PAIRS * b + p + 1)
                        for u in range(2):
                            ins = dve.tensor_tensor(o[:, par, :, (2 * p + u) * DH:(2 * p + u + 1) * DH],
                                                    pv_ps[:, 2 * u:2 * u + 2, 0:DH],
                                                    rsum[:, p % 2, 2 * u:2 * u + 2].unsqueeze(2).to_broadcast([P, 2, DH]), ALU.mult)
                        ins.then_inc(o_ready, 1)
                    return body

                def add(b, par, r, again):
                    dve.wait_ge(biased, b + 1)
                    dve.wait_ge(out_psum, b + 1)
                    both = resid[:, bass.ds(2 * b, 2), :].rearrange("p h d -> p (h d)")
                    dve.tensor_tensor(both, both, bank[0], ALU.add).then_inc(added, 1)
                    hold(dve, added, b + 1)
                    for h in range(2):
                        dve.bn_stats(stats[:, 2 * b + h, :], resid[:, 2 * b + h, :])

                heads = []
                for p in range(PAIRS):
                    heads += [(1, maxima(2 * p)), (1, maxima(2 * p + 1))] + [(0, normalise)] * (p == 0) + [(3, add)] * (p == 2)
                    heads += [(2, normal(p - 1))] * (p > 0)
                staged(dve, B, (1, low_x), (3, normal(PAIRS - 1)), (1, lows), *heads, (1, split))


def moe(nc, psum, resid, mv, stats, ident, roots, phiT, phi_b, expert_w, expert_b, consts, out):
    PHI = 64.0
    Q = 4
    QS = SLOTS // Q
    QE = NE // Q
    ST = SLOTS // P
    EP = P // PS
    G = 8
    GT = T // G
    GW = GT * P
    with ExitStack() as outer:
        def sb(name, shape, dt=F32):
            return outer.enter_context(nc.sbuf_tensor("m_" + name, shape, dt))

        def sem(name):
            return outer.enter_context(nc.semaphore("m_" + name))
        xTh, xTl = sb("xTh", [P, DC, T * P], F16), sb("xTl", [P, DC, T * P], F16)
        ph, pl = sb("ph", [P, DC, SLOTS], F16), sb("pl", [P, DC, SLOTS], F16)
        shiftC = sb("shiftC", [2 * PS, T * P], BF16)
        phib_col = sb("phib_col", [P, ST])
        yh, yl = sb("yh", [P, ST, D], F16), sb("yl", [P, ST, D], F16)
        gather_slots(nc, psum, resid, mv, stats, ident, roots, phiT, phi_b, expert_w, expert_b, consts,
                     xTh, xTl, ph, pl, shiftC, phib_col, yh, yl, PHI, Q, QS, QE, ST, EP)
        selC_f = sb("selC_f", [2 * PS, P])
        selC = sb("selC", [2 * PS, P], BF16)
        sel_sum = sb("sel_sum", [P, P])
        e = sb("e", [P, 2, ST, GW])
        total = sb("total", [P, 2, GW])
        inv = sb("inv", [P, 2, GW])
        ch, cl = sb("ch", [P, 4, GW], F16), sb("cl", [P, 4, GW], F16)
        c_in, selC_ready = sem("c_in"), sem("selC_ready")
        lt_psum, ex_ready, tot_ready, sum_psum, inv_ready = (
            sem("lt_psum"), sem("ex_ready"), sem("tot_ready"), sem("sum_psum"), sem("inv_ready"))
        norm_ready, ch_ready, cl_ready, y_step, y_added, stored = (
            sem("norm_ready"), sem("ch_ready"), sem("cl_ready"), sem("y_step"), sem("y_added"), sem("stored"))
        LT = 3
        lt_ps = [psum[:, n, :] for n in range(LT)]
        sum_ps = psum[:, LT, :]
        y_ps = psum[:, LT + 1:8, :].rearrange("p (g a) (t d) -> p g (a t) d", g=2, d=D)

        def behind(by, at, step):
            return (1, step(at - by)) if at >= by else (2, step(ST + at - by))

        with nc.Block() as block:
            @block.sync
            def _(sp):
                sp.dma_start(selC_f[:], consts["selC"]).then_inc(c_in, 16)
                sp.dma_start(sel_sum[:], consts["sel_sum"]).then_inc(c_in, 16)
                rows = out.rearrange("b (h p) d -> p (b h) d", p=P)

                def store(b, par, r, again):
                    sp.wait_ge(y_added, 2 * b + 2)
                    sp.dma_start(rows[:, bass.ds(GT * b, GT), :], resid[:, bass.ds(GT * b, GT), :]).then_inc(stored, 16)
                pairs(sp, G, store)
                sp.wait_ge(stored, 16 * G)

            @block.tensor
            def _(pe):
                pe.wait_ge(c_in, 32)
                pe.wait_ge(selC_ready, 1)

                def logits(s):
                    def body(b, par, r, again):
                        if late(ST * b + s, LT):
                            pe.wait_ge(ex_ready, ST * b + s - LT + (2 if par == 0 and s < 2 else 1))
                        dst, slots, toks = lt_ps[(ST * par + s) % LT], slice(s * P, (s + 1) * P), bass.ds(GW * b, GW)
                        for k in range(DC):
                            pe.matmul(dst, ph[:, k, slots], xTh[:, k, toks], start=(k == 0), stop=False)
                            pe.matmul(dst, ph[:, k, slots], xTl[:, k, toks], start=False, stop=False)
                            pe.matmul(dst, pl[:, k, slots], xTh[:, k, toks], start=False, stop=False)
                        pe.matmul(dst, selC[:], shiftC[:, toks], start=False, stop=True).then_inc(lt_psum, 1)
                    return body

                def spread(s):
                    def body(b, par, r, again):
                        pe.wait_ge(cl_ready, ST * b + s + 1)
                        if s == 0 and late(b, 2):
                            pe.wait_ge(y_added, 2 * b - 2)
                        for t in range(GT):
                            toks = slice(t * P, (t + 1) * P)
                            pe.matmul(y_ps[:, par, t, :], ch[:, s % 4, toks], yh[:, s, :], start=(s == 0 and t % 2 == 0),
                                      stop=False, skip_group_check=True)
                            pe.matmul(y_ps[:, par, t, :], ch[:, s % 4, toks], yl[:, s, :], start=False, stop=False, skip_group_check=True)
                            ins = pe.matmul(y_ps[:, par, t, :], cl[:, s % 4, toks], yh[:, s, :], start=False, stop=(s == ST - 1),
                                            skip_group_check=True)
                        ins.then_inc(y_step, 1)
                    return body

                def sums(b, par, r, again):
                    pe.wait_ge(tot_ready, ST * b + ST)
                    if late(b, 1):
                        pe.wait_ge(inv_ready, b)
                    pe.matmul(sum_ps, sel_sum[:], total[:, (ST - 1) % 2, :], start=True, stop=True).then_inc(sum_psum, 1)
                steps = []
                for s in range(ST):
                    steps += [(0, logits(s))] + [(1, sums)] * (s == 1) + [behind(4, s, spread)]
                staged(pe, G, *steps)

            @block.scalar
            def _(act):
                def exponential(s):
                    def body(b, par, r, again):
                        act.wait_ge(lt_psum, ST * b + s + 1)
                        if late(b, 2):
                            act.wait_ge(cl_ready, ST * (b - 2) + s + 1)
                        act.activation(e[:, par, s, :], lt_ps[(ST * par + s) % LT], ACT.Exp, bias=phib_col[:, s:s + 1],
                                       scale=1.0 / PHI).then_inc(ex_ready, 1)
                    return body

                def high(s):
                    def body(b, par, r, again):
                        act.wait_ge(norm_ready, ST * b + s + 1)
                        if late(ST * b + s, 4):
                            act.wait_ge(y_step, ST * b + s - 3)
                        act.activation(ch[:, s % 4, :], e[:, par, s, :], ACT.Copy).then_inc(ch_ready, 1)
                    return body
                steps = []
                for s in range(ST):
                    steps += [behind(3, s, high), (0, exponential(s))]
                staged(act, G, *steps)

            @block.gpsimd
            def _(pool):
                def low(s):
                    def body(b, par, r, again):
                        pool.wait_ge(ch_ready, ST * b + s + 1)
                        pool.tensor_tensor(cl[:, s % 4, :], e[:, par, s, :], ch[:, s % 4, :], ALU.subtract).then_inc(cl_ready, 1)
                    return body
                staged(pool, G, *[(0, low(s)) for s in range(ST)])

            @block.vector
            def _(dve):
                dve.wait_ge(c_in, 32)
                dve.tensor_copy(selC[:], selC_f[:]).then_inc(selC_ready, 1)

                def accumulate(s):
                    def body(b, par, r, again):
                        if s == 0:
                            return
                        dve.wait_ge(ex_ready, ST * b + s + 1)
                        before = e[:, par, 0, :] if s == 1 else total[:, (s - 1) % 2, :]
                        if s > 1:
                            dve.wait_ge(tot_ready, ST * b + s)
                        if s == 1 and late(b, 1):
                            dve.wait_ge(sum_psum, b)
                        ins = dve.tensor_tensor(total[:, s % 2, :], before, e[:, par, s, :], ALU.add)
                        ins.then_inc(tot_ready, 2 if s == 1 else 1)
                    return body

                def normalise(s):
                    def body(b, par, r, again):
                        if s == 0:
                            dve.wait_ge(inv_ready, b + 1)
                        dve.tensor_tensor(e[:, par, s, :], e[:, par, s, :], inv[:, par, :], ALU.mult).then_inc(norm_ready, 1)
                    return body

                def invert(b, par, r, again):
                    dve.wait_ge(sum_psum, b + 1)
                    dve.reciprocal(inv[:, par, :], sum_ps).then_inc(inv_ready, 1)

                def add(b, par, r, again):
                    dve.wait_ge(y_step, ST * (b + 1))
                    for t in range(2):
                        both = resid[:, bass.ds(GT * b + 2 * t, 2), :]
                        dve.tensor_tensor(both, both, y_ps[:, par, 2 * t:2 * t + 2, :], ALU.add).then_inc(y_added, 1)
                steps = []
                for s in range(ST):
                    steps += [(0, accumulate(s))] + [(1, invert)] * (s == 1) + [behind(2, s, normalise)] + [(2, add)] * (s == 4)
                staged(dve, G, *steps)


def gather_slots(nc, psum, resid, mv, stats, ident, roots, phiT, phi_b, expert_w, expert_b, consts,
                 xTh, xTl, ph, pl, shiftC, phib_col, yh, yl, PHI, Q, QS, QE, ST, EP):
    with ExitStack() as c:
        def sb(name, shape, dt=F32):
            return c.enter_context(nc.sbuf_tensor("g_" + name, shape, dt))

        def sem(name):
            return c.enter_context(nc.semaphore("g_" + name))
        slots_in = sb("slots_in", [P, DC, SLOTS])
        cmax = sb("cmax", [P, T, Q, PS])
        with ExitStack() as c1:
            def sb1(name, shape, dt=F32):
                return c1.enter_context(nc.sbuf_tensor("g_" + name, shape, dt))
            xh, xl = sb1("xh", [P, T, D], F16), sb1("xl", [P, T, D], F16)
            identb = sb1("identb", [P, P], BF16)
            rstd, rtmp, rroot = sb1("rstd", [P, T]), sb1("rtmp", [P, T]), sb1("rroot", [P, T])
            xn = sb1("xn", [P, 2, D])
            pb_rows = sb1("pb_rows", [SLOTS // P, P])
            pb_parts = sb1("pb_parts", [SLOTS // P, 3, P], BF16)
            pb3 = sb1("pb3", [3, SLOTS], BF16)
            ones3 = sb1("ones3", [3, P], BF16)
            selD_f = sb1("selD_f", [2 * QE, QS])
            selD = sb1("selD", [2 * QE, QS], BF16)
            top = sb1("top", [P, 2, QE])
            sp_ = sb1("sp", [P, 2, 2 * QE], BF16)
            spT = sb1("spT", [2 * QE, 2, P], BF16)
            e = sb1("e", [P, 4, QS])
            esum, einv = sb1("esum", [P, 2, QE]), sb1("einv", [P, 2, QE])
            dh, dl = sb1("dh", [P, 4, QS], F16), sb1("dl", [P, 4, QS], F16)
            phi_f = slots_in

            w_in, parts_in, setup = sem("w_in"), sem("parts_in"), sem("setup")
            own_steps, phi_ready, parts_ready = (
                sem("own_steps"), sem("phi_ready"), sem("parts_ready"))
            xn_ready, xh_ready, x_psum, xTh_ready, xl_ready, xTl_ready = (
                sem("xn_ready"), sem("xh_ready"), sem("x_psum"), sem("xTh_ready"), sem("xl_ready"), sem("xTl_ready"))
            log_psum, top_ready, hi_ready, sp_ready, spT_psum, spT_ready, shift_psum = (
                sem("log_psum"), sem("top_ready"), sem("hi_ready"), sem("sp_ready"), sem("spT_psum"), sem("spT_ready"), sem("shift_psum"))
            ex_ready, esum_ready, einv_ready, dn_ready, dh_ready, dl_ready, slot_psum, slot_taken = (
                sem("ex_ready"), sem("esum_ready"), sem("einv_ready"), sem("dn_ready"), sem("dh_ready"), sem("dl_ready"),
                sem("slot_psum"), sem("slot_taken"))
            x_ps = [psum[:, n, 0:D] for n in range(2)]
            log_ps = [psum[:, n, :] for n in range(4)]
            spT_ps = psum[:, 4, :].bitcast(BF16)
            slot_ps = [psum[:, 5, :], psum[:, 6, :]]

            with nc.Block() as block:
                @block.sync
                def _(sp):
                    sp.dma_start(phi_f[:], phiT.rearrange("(c p) n -> p c n", p=P)).then_inc(w_in, 16)
                    sp.dma_start(pb_rows[:], phi_b).then_inc(w_in, 16)
                    sp.dma_start(selD_f[:], consts["selD"]).then_inc(w_in, 16)
                    sp.dma_start(phib_col[:], consts["phi_b_col"]).then_inc(w_in, 16)
                    sp.wait_ge(parts_ready, 3)
                    for n in range(3):
                        sp.dma_start(pb3[n:n + 1, :].rearrange("o (s p) -> o s p", p=P), pb_parts[:, n, :]).then_inc(parts_in, 16)

                @block.tensor
                def _(pe):
                    def turn(b, par, r, again):
                        pe.wait_ge(xn_ready, b + 1)
                        if again:
                            pe.wait_ge(xTl_ready, b - 1)
                        for k in range(DC):
                            ins = pe.transpose(x_ps[par][:, k * P:(k + 1) * P], xn[:, par, k * P:(k + 1) * P], ident[:])
                        ins.then_inc(x_psum, 1)
                    pairs(pe, T, turn)
                    pe.wait_ge(xTl_ready, T)
                    pe.wait_ge(setup, 3)
                    pe.wait_ge(phi_ready, 2)
                    pe.wait_ge(xl_ready, T)
                    pe.wait_ge(parts_in, 48)

                    with pe.Fori(0, Q) as q:
                        def logits(t, slot, r, again):
                            u = T * q + t
                            if late(t, 4):
                                pe.wait_ge(ex_ready, u - 3)
                            dst, toks, cols = log_ps[slot], bass.ds(t * P, P), bass.ds(q * QS, QS)
                            for k in range(DC):
                                pe.matmul(dst, xTh[:, k, toks], ph[:, k, cols], start=(k == 0), stop=False)
                                pe.matmul(dst, xTh[:, k, toks], pl[:, k, cols], start=False, stop=False)
                                pe.matmul(dst, xTl[:, k, toks], ph[:, k, cols], start=False, stop=False)
                            pe.matmul(dst, ones3[:], pb3[:, cols], start=False, stop=True).then_inc(log_psum, 1)

                        def turn_tops(t, slot, r, again):
                            u = T * q + t
                            pe.wait_ge(sp_ready, u + 1)
                            if late(t, 1):
                                pe.wait_ge(spT_ready, u)
                            pe.transpose(spT_ps[0:2 * QE, 0:P], sp_[:, slot % 2, :], identb[:]).then_inc(spT_psum, 1)

                        def gather(t, slot, r, again):
                            u = T * q + t
                            pe.wait_ge(dl_ready, u + 1)
                            if not late(t, 1):
                                pe.wait_ge(slot_taken, 2 * q + 1)
                            first, last = isinstance(t, int) and t == 0, isinstance(t, int) and t == T - 1
                            for k in range(DC):
                                high = xh[:, t, k * P:(k + 1) * P]
                                pe.matmul(slot_ps[k], high, dh[:, slot, :], start=first, stop=False, skip_group_check=True)
                                pe.matmul(slot_ps[k], high, dl[:, slot, :], start=False, stop=False, skip_group_check=True)
                                ins = pe.matmul(slot_ps[k], xl[:, t, k * P:(k + 1) * P], dh[:, slot, :], start=False, stop=last,
                                                skip_group_check=True)
                            ins.then_inc(slot_psum, 1)

                        def shift(t, slot, r, again):
                            pe.wait_ge(spT_ready, T * q + t + 1)
                            pe.matmul(log_ps[slot], spT[:, slot % 2, :], selD[:], start=False, stop=True,
                                      skip_group_check=True).then_inc(shift_psum, 1)
                        staged(pe, T, (0, logits), (1, turn_tops), (4, gather), (1, shift), unroll=4)

                @block.scalar
                def _(act):
                    rstd_root(act, roots, 4, mv[:, :, 1], rroot[:])

                    def highs(b, par, r, again):
                        hold(act, xn_ready, b + 1)
                        act.activation(xh[:, b, :], xn[:, par, :], ACT.Copy).then_inc(xh_ready, 1)
                        hold(act, x_psum, b + 1)
                        act.activation(xTh[:, :, bass.ds(b * P, P)], x_ps[par].rearrange("p (c t) -> p c t", c=DC),
                                       ACT.Copy).then_inc(xTh_ready, 1)
                    pairs(act, T, highs)

                    with act.Fori(0, Q) as q:
                        def take_tops(t, slot, r, again):
                            act.wait_ge(spT_psum, T * q + t + 1)
                            act.activation(spT[:, slot % 2, :], spT_ps[0:2 * QE, 0:P], ACT.Copy).then_inc(spT_ready, 1)

                        def exponential(t, slot, r, again):
                            u = T * q + t
                            act.wait_ge(shift_psum, u + 1)
                            if late(t, 4):
                                act.wait_ge(dl_ready, u - 3)
                            act.activation(e[:, slot, :], log_ps[slot], ACT.Exp, scale=1.0 / PHI).then_inc(ex_ready, 1)

                        def high(t, slot, r, again):
                            u = T * q + t
                            act.wait_ge(dn_ready, u + 1)
                            if late(t, 4):
                                act.wait_ge(slot_psum, u - 3)
                            act.activation(dh[:, slot, :], e[:, slot, :], ACT.Copy).then_inc(dh_ready, 1)
                        staged(act, T, (0, take_tops), (0, exponential), (1, high), unroll=4)

                @block.gpsimd
                def _(pool):
                    def low_x(b, par, r, again):
                        pool.wait_ge(xh_ready, b + 1)
                        pool.tensor_tensor(xl[:, b, :], xn[:, par, :], xh[:, b, :], ALU.subtract).then_inc(xl_ready, 1)
                    pairs(pool, T, low_x)

                    with pool.Fori(0, Q) as q:
                        def product(t, slot, r, again):
                            u = T * q + t
                            pool.wait_ge(einv_ready, u + 1)
                            pool.tensor_tensor(e[:, slot, :].rearrange("p (n s) -> p n s", s=PS),
                                               e[:, slot, :].rearrange("p (n s) -> p n s", s=PS),
                                               einv[:, slot % 2, :].unsqueeze(2).to_broadcast([P, QE, PS]),
                                               ALU.mult).then_inc(dn_ready, 1)

                        def low(t, slot, r, again):
                            pool.wait_ge(dh_ready, T * q + t + 1)
                            pool.tensor_tensor(dl[:, slot, :], e[:, slot, :], dh[:, slot, :], ALU.subtract).then_inc(dl_ready, 1)
                        staged(pool, T, (0, product), (1, low), unroll=4)

                @block.vector
                def _(dve):
                    own = Steps(dve, own_steps)
                    dve.sem_inc(slot_taken, 1)
                    dve.memset(ones3[:], 1.0).then_inc(setup, 1)
                    dve.tensor_copy(identb[:], ident[:]).then_inc(setup, 1)
                    moments(own, dve, stats, mv, rtmp[:])
                    rstd_of(own, dve, roots, 4, mv[:, :, 1], rroot[:], rstd[:], rtmp[:])

                    def parts(b, par, r, again):
                        if late(b, 2):
                            dve.wait_ge(xh_ready, b - 1)
                            dve.wait_ge(x_psum, b - 1)
                            dve.wait_ge(xl_ready, b - 1)
                        dve.tensor_scalar(xn[:, par, :], resid[:, b, :], mv[:, b, 0:1], rstd[:, bass.ds(b, 1)],
                                          ALU.subtract, ALU.mult).then_inc(xn_ready, 1)

                    def lows(b, par, r, again):
                        dve.wait_ge(xTh_ready, b + 1)
                        toks = bass.ds(b * P, P)
                        dve.tensor_tensor(xTl[:, :, toks], x_ps[par].rearrange("p (c t) -> p c t", c=DC), xTh[:, :, toks],
                                          ALU.subtract).then_inc(xTl_ready, 1)
                    staged(dve, T, (0, parts), (1, lows))
                    dve.wait_ge(w_in, 64)
                    dve.tensor_copy(selD[:], selD_f[:]).then_inc(setup, 1)
                    own.then(dve.tensor_scalar(pb_rows[:], pb_rows[:], PHI, None, ALU.mult))
                    for n in range(3):
                        dve.tensor_copy(pb_parts[:, n, :], pb_rows[:]).then_inc(parts_ready, 1)
                        if n < 2:
                            dve.wait_ge(parts_ready, n + 1)
                            own.then(dve.tensor_tensor(pb_rows[:], pb_rows[:], pb_parts[:, n, :], ALU.subtract))
                    for k in range(DC):
                        own.then(dve.tensor_scalar(ph[:, k, :], phi_f[:, k, :], PHI, None, ALU.mult))
                        dve.scalar_tensor_tensor(out=pl[:, k, :], in0=phi_f[:, k, :], scalar=PHI, in1=ph[:, k, :],
                                                 op0=ALU.mult, op1=ALU.subtract).then_inc(phi_ready, 1)

                    dve.wait_ge(phi_ready, 2)

                    with dve.Fori(0, Q) as q:
                        def tops(t, slot, r, again):
                            u = T * q + t
                            par = slot % 2
                            dve.wait_ge(log_psum, u + 1)
                            dve.tensor_reduce(top[:, par, :], log_ps[slot].rearrange("p (n s) -> p n s", s=PS),
                                              AX.X, ALU.max).then_inc(top_ready, 1)
                            dve.tensor_reduce(cmax[:, t, q, :], log_ps[slot].rearrange("p (n s) -> p s n", s=PS),
                                              AX.X, ALU.max)
                            dve.wait_ge(top_ready, u + 1)
                            if late(t, 2):
                                dve.wait_ge(spT_psum, u - 1)
                            dve.tensor_scalar(sp_[:, par, 0:QE], top[:, par, :], -1.0, None, ALU.mult).then_inc(hi_ready, 1)
                            dve.wait_ge(hi_ready, u + 1)
                            dve.scalar_tensor_tensor(out=sp_[:, par, QE:], in0=top[:, par, :], scalar=-1.0,
                                                     in1=sp_[:, par, 0:QE], op0=ALU.mult, op1=ALU.subtract).then_inc(sp_ready, 1)

                        def sums(t, slot, r, again):
                            u = T * q + t
                            par = slot % 2
                            dve.wait_ge(ex_ready, u + 1)
                            dve.tensor_reduce(esum[:, par, :], e[:, slot, :].rearrange("p (n s) -> p n s", s=PS),
                                              AX.X, ALU.add).then_inc(esum_ready, 1)
                            dve.wait_ge(esum_ready, u + 1)
                            if late(t, 2):
                                dve.wait_ge(dn_ready, u - 1)
                            dve.reciprocal(einv[:, par, :], esum[:, par, :]).then_inc(einv_ready, 1)
                        staged(dve, T, (0, tops), (1, sums), unroll=4)
                        for k in range(DC):
                            dve.wait_ge(slot_psum, T * (q + 1))
                            dve.tensor_copy(slots_in[:, k, bass.ds(q * QS, QS)], slot_ps[k]).then_inc(slot_taken, 1)

        experts(nc, psum, ident, roots, slots_in, cmax, expert_w, expert_b, consts, shiftC, yh, yl, Q, ST, EP)


def experts(nc, psum, ident, roots, slots_in, cmax, expert_w, expert_b, consts, shiftC, yh, yl, Q, ST, EP):
    RING = 4
    with ExitStack() as c:
        def sb(name, shape, dt=F32):
            return c.enter_context(nc.sbuf_tensor("x_" + name, shape, dt))

        def sem(name):
            return c.enter_context(nc.semaphore("x_" + name))
        w = sb("w", [P, RING, EP, DC, D])
        bias = sb("bias", [EP, RING, D])
        esel = sb("esel", [EP, P])
        identb = sb("identb", [P, P], BF16)
        xT = sb("xT", [P, 2, DC, P])
        slots = sb("slots", [P, ST, D])
        smv, sstats = sb("smv", [P, ST, 2]), sb("sstats", [P, ST, 6])
        rstd, rtmp, rroot = sb("rstd", [P, ST]), sb("rtmp", [P, ST]), sb("rroot", [P, ST])
        a = sb("a", [P, 2, D])
        th = sb("th", [P, 2, D])
        thT = sb("thT", [P, 2, D])
        y = sb("y", [P, 2, D])
        cm = sb("cm", [P, T, PS])
        cs2 = cmax[:].rearrange("p t q s -> p (t q s)")[:, 0:T * PS].bitcast(BF16).rearrange("p (t u s) -> p t u s", u=2, s=2 * PS)
        cs = cs2.rearrange("p t u s -> p (t u) s")
        w_in = [sem(f"w_in{n}") for n in range(RING)]
        b_in, setup, own_steps = sem("b_in"), sem("setup"), sem("own_steps")
        copied, slot_psum, clipped, cs_ready, cs_psum, cs_taken = (
            sem("copied"), sem("slot_psum"), sem("clipped"), sem("cs_ready"), sem("cs_psum"), sem("cs_taken"))
        a_ready, th_ready, th_psum, thT_ready, y_psum, y_ready, yh_ready, yl_ready = (
            sem("a_ready"), sem("th_ready"), sem("th_psum"), sem("thT_ready"), sem("y_psum"), sem("y_ready"), sem("yh_ready"), sem("yl_ready"))
        bank = [psum[:, n, 0:D] for n in range(8)]

        with nc.Block() as block:
            @block.sync
            def _(sp):
                sp.dma_start(esel[:], consts["esel"]).then_inc(b_in, 16)

                def load(s, slot, r, again):
                    if late(s, RING):
                        sp.wait_ge(y_psum, s - RING + 1)
                    sp.dma_start(bias[:, slot, :], expert_b[bass.ds(EP * s, EP), :]).then_inc(w_in[slot], 16)
                    for j in range(EP):
                        sp.dma_start(w[:, slot, j], expert_w[EP * s + j].rearrange("(c p) n -> p c n", p=P)).then_inc(w_in[slot], 16)
                staged(sp, ST, (0, load), unroll=RING)

            @block.tensor
            def _(pe):
                pe.wait_ge(setup, 1)

                def turn(s, par, r, again):
                    pe.wait_ge(copied, s + 1)
                    if again:
                        pe.wait_ge(clipped, s - 1)
                    for k in range(DC):
                        ins = pe.transpose(bank[par][:, k * P:(k + 1) * P], xT[:, par, k, :], ident[:])
                    ins.then_inc(slot_psum, 1)
                pairs(pe, ST, turn)
                pe.wait_ge(cs_ready, 1)

                def turn_max(t, par, r, again):
                    if again:
                        pe.wait_ge(cs_taken, 2 * t - 2)
                    pe.transpose(psum[:, 2 + par, :].bitcast(BF16)[:, 0:P],
                                 cs2[:, t].rearrange("p t s -> p (t s)"), identb[:]).then_inc(cs_psum, 1)
                pairs(pe, T // 2, turn_max)
                pe.wait_ge(b_in, 16)

                def run(s, slot, r, again):
                    par = slot % 2
                    pe.wait_ge(th_ready, s + 1)
                    if late(s, 2):
                        pe.wait_ge(thT_ready, s - 1)
                    for k in range(DC):
                        ins = pe.transpose(bank[4 + par][:, k * P:(k + 1) * P], th[:, par, k * P:(k + 1) * P], ident[:])
                    ins.then_inc(th_psum, 1)
                    if late(s, 2):
                        pe.wait_ge(y_ready, s - 1)
                    pe.wait_ge(w_in[slot], 16 * (EP + 1) * (r + 1))
                    pe.matmul(bank[6 + par], esel[:], bias[:, slot, :], start=True, stop=False, skip_group_check=True)
                    pe.wait_ge(thT_ready, s + 1)
                    for j in range(EP):
                        for k in range(DC):
                            ins = pe.matmul(bank[6 + par][j * PS:(j + 1) * PS, :], thT[:, par, k * P + j * PS:k * P + (j + 1) * PS],
                                            w[:, slot, j, k, :], start=False, stop=(k == DC - 1), skip_group_check=True)
                    ins.then_inc(y_psum, 1)
                staged(pe, ST, (0, run), unroll=RING)

            @block.scalar
            def _(act):
                def copy(s, par, r, again):
                    if again:
                        act.wait_ge(slot_psum, s - 1)
                    act.activation(xT[:, par], slots_in[:, :, bass.ds(s * P, P)], ACT.Copy).then_inc(copied, 1)
                pairs(act, ST, copy)

                def take(t, par, r, again):
                    hold(act, cs_psum, t + 1)
                    for n in range(2):
                        act.activation(shiftC[:, bass.ds((2 * t + n) * P, P)],
                                       psum[:, 2 + par, :].bitcast(BF16)[n * 2 * PS:(n + 1) * 2 * PS, 0:P],
                                       ACT.Copy).then_inc(cs_taken, 1)
                pairs(act, T // 2, take)
                rstd_root(act, roots, 5, smv[:, :, 1], rroot[:])

                def tanh(s, par, r, again):
                    act.wait_ge(a_ready, s + 1)
                    if again:
                        act.wait_ge(th_psum, s - 1)
                    act.activation(th[:, par, :], a[:, par, :], ACT.Tanh).then_inc(th_ready, 1)

                def turned(s, par, r, again):
                    act.wait_ge(th_psum, s + 1)
                    if again:
                        act.wait_ge(y_psum, s - 1)
                    act.activation(thT[:, par, :], bank[4 + par], ACT.Copy).then_inc(thT_ready, 1)

                def take_y(s, par, r, again):
                    act.wait_ge(y_psum, s + 1)
                    if again:
                        act.wait_ge(yl_ready, s - 1)
                    act.activation(y[:, par, :], bank[6 + par], ACT.Copy).then_inc(y_ready, 1)
                staged(act, ST, (0, tanh), (0, turned), (1, take_y))

            @block.vector
            def _(dve):
                own = Steps(dve, own_steps)
                dve.tensor_copy(identb[:], ident[:]).then_inc(setup, 1)
                own.then(dve.tensor_reduce(cm[:], cmax[:].rearrange("p t q s -> p t s q"), AX.X, ALU.max))
                own.then(dve.tensor_scalar(cs[:, :, 0:PS], cm[:], -1.0, None, ALU.mult))
                dve.scalar_tensor_tensor(out=cs[:, :, PS:], in0=cm[:], scalar=-1.0, in1=cs[:, :, 0:PS],
                                         op0=ALU.mult, op1=ALU.subtract).then_inc(cs_ready, 1)

                def clip(s, par, r, again):
                    dve.wait_ge(slot_psum, s + 1)
                    dve.tensor_scalar(slots[:, s, :], bank[par], -33000.0, 65000.0, ALU.max, ALU.min).then_inc(clipped, 1)
                    hold(dve, clipped, s + 1)
                    dve.bn_stats(sstats[:, s, :], slots[:, s, :])
                pairs(dve, ST, clip)
                own.then(dve.memset(a[:], 0.0))
                moments(own, dve, sstats, smv, rtmp[:])
                rstd_of(own, dve, roots, 5, smv[:, :, 1], rroot[:], rstd[:], rtmp[:])

                def normalise(s, par, r, again):
                    if again:
                        dve.wait_ge(th_ready, s - 1)
                    dve.tensor_scalar(a[:, par, :], slots[:, s, :], smv[:, s, 0:1], rstd[:, bass.ds(s, 1)],
                                      ALU.subtract, ALU.mult).then_inc(a_ready, 1)

                def parts(s, par, r, again):
                    dve.wait_ge(y_ready, s + 1)
                    dve.tensor_copy(yh[:, s, :], y[:, par, :]).then_inc(yh_ready, 1)
                    dve.wait_ge(yh_ready, s + 1)
                    dve.tensor_tensor(yl[:, s, :], y[:, par, :], yh[:, s, :], ALU.subtract).then_inc(yl_ready, 1)
                staged(dve, ST, (0, normalise), (2, parts))


def kernel(**inputs):
    import numpy as np
    import concourse.bacc as bacc
    from concourse.bass_utils import run_bass_kernel_spmd

    f32 = np.float32
    g = {k: np.asarray(v) for k, v in inputs.items()}
    lane = np.arange(P) % LANES
    ends = np.zeros((P, BW + 1), f32)
    ends[lane == 0, S - (BLK - 1) * BW] = 1.0
    arrays = {
        "x": g["x"], "ctx": g["ctx_1024"], "ctxT": g["ctx_1024"].transpose(0, 2, 1),
        "w_gateT": g["L0_ffn_w_gate"].T, "w_upT": g["L0_ffn_w_up"].T, "w_downT": g["L0_ffn_w_down"].T,
        "wq1": g["L1_xattn_Wq1"], "wk1": g["L1_xattn_Wk1"], "wv1": g["L1_xattn_Wv1"],
        "wk2": g["L1_xattn_Wk2"], "wv2": g["L1_xattn_Wv2"], "wo": g["L1_xattn_Wo"], "bo": np.broadcast_to(g["L1_xattn_bo"], (P, D)),
        "phiT": g["L1_ffn_phi_w"].T, "phi_b": g["L1_ffn_phi_b"].reshape(SLOTS // P, P),
        "expert_w": g["L1_ffn_expert_w"], "expert_b": g["L1_ffn_expert_b"],
        "ident_c": np.eye(P, dtype=f32),
        "lane_start_c": np.where(lane == BLK - 1, 0.0, BIG).astype(f32)[:, None],
        "path_end_c": ends,
        "head_sel_c": np.kron(np.tile(np.eye(HEADS, dtype=f32), (2, 1)), np.ones((1, P), f32)),
    }
    shaped = {
        "selD": np.kron(np.tile(np.eye(NE // 4, dtype=f32), (2, 1)), np.ones((1, PS), f32)),
        "selC": np.tile(np.eye(PS, dtype=f32), (2, P // PS)),
        "sel_sum": np.tile(np.eye(PS, dtype=f32), (P // PS, P // PS)),
        "esel": np.kron(np.eye(P // PS, dtype=f32), np.ones((1, PS), f32)),
        "phi_b_col": g["L1_ffn_phi_b"].reshape(SLOTS // P, P).T,
    }
    arrays.update(shaped)
    arrays = {f"in_{k}": np.ascontiguousarray(v) for k, v in arrays.items()}
    nc = bacc.Bacc("TRN2", target_bir_lowering=False, num_devices=1)
    args = [nc.dram_tensor(k, v.shape, mybir.dt.from_np(v.dtype), kind="ExternalInput").ap() for k, v in arrays.items()]
    consts = dict(zip(shaped, args[-len(shaped):]))
    args = args[:-len(shaped)]
    out = nc.dram_tensor("out", (B, S, D), F32, kind="ExternalOutput").ap()
    program(nc, *args, consts, out, 0)
    r = run_bass_kernel_spmd(nc, [arrays], core_ids=[0])
    return r.results[0]["out"]
```
